# Optimizing a Trainium2 kernel written in Bass

```python
import numpy as np
import jax
import jax.numpy as jnp

def _softmax(x, axis=-1):
    return jax.nn.softmax(x, axis=axis)

def _gelu(x):
    return jax.nn.gelu(x, approximate=True)

def _silu(x):
    return jax.nn.silu(x)

def _sigmoid(x):
    return jax.nn.sigmoid(x)

def _layernorm(x, axis=-1, eps=1e-05):
    m = jnp.mean(x, axis=axis, keepdims=True)
    v = jnp.var(x, axis=axis, keepdims=True)
    return (x - m) / jnp.sqrt(v + eps)

def _scatter_add(tgt, idx, src, axis=0):
    return tgt.at[idx].add(src)

def _segment_sum(src, seg, n):
    return jax.ops.segment_sum(src, seg, n)
kernel_name = 'mk_seq_postln_d2_jaxref_r8_9cd775'

def setup_inputs(seed: int=0):
    np.random.seed(seed)
    _w = jnp.asarray

    def _L0_attn_setup():
        import jax, jax.numpy as jnp
        import numpy as np
        import math
        N_HEADS, D_HEAD, D_MODEL = (16, 64, 128)
        B, S = (4, 256)
        NEG_MASK = -100000.0
        key = jax.random.key(seed)
        ks = jax.random.split(key, 9)
        bound = math.sqrt(6.0 / (D_MODEL + D_HEAD))

        def w(k):
            return jax.random.uniform(k, (N_HEADS, D_MODEL, D_HEAD), jnp.float32, -bound, bound)
        return {'x': jax.random.normal(ks[0], (B, S, D_MODEL), jnp.float32), 'Q_w': w(ks[1]), 'Q_b': jnp.zeros((N_HEADS, D_HEAD), jnp.float32), 'K_w': w(ks[2]), 'K_b': jnp.zeros((N_HEADS, D_HEAD), jnp.float32), 'V_w': w(ks[3]), 'V_b': jnp.zeros((N_HEADS, D_HEAD), jnp.float32), 'O_w': jax.random.uniform(ks[4], (N_HEADS, D_HEAD, D_MODEL), jnp.float32, -bound, bound), 'O_b': jnp.zeros((D_MODEL,), jnp.float32)}
    _L0_attn_in = _L0_attn_setup()

    def _L0_ffn_setup():
        import jax, jax.numpy as jnp
        import numpy as np
        D_IN, D_HID = (128, 512)

        def _ternary(key, shape):
            return jax.random.randint(key, shape, -1, 2).astype(jnp.float32)

        def _tlin(x, w, s):
            return jnp.einsum('bsi,oi->bso', x, w) * s
        key = jax.random.key(seed)
        ks = jax.random.split(key, 12)
        inv = lambda fan: 1.0 / np.sqrt(fan).astype(np.float32)
        return {'x': jax.random.normal(ks[0], (4, 256, D_IN), dtype=jnp.float32), 'w1_w': _ternary(ks[1], (D_HID, D_IN)), 'w1_s': jax.random.uniform(ks[2], (D_HID,), dtype=jnp.float32) * inv(D_IN), 'w2_w': _ternary(ks[3], (D_HID, D_IN)), 'w2_s': jax.random.uniform(ks[4], (D_HID,), dtype=jnp.float32) * inv(D_IN), 'h1_w': _ternary(ks[5], (D_HID, D_HID)), 'h1_s': jax.random.uniform(ks[6], (D_HID,), dtype=jnp.float32) * inv(D_HID), 'h2_w': _ternary(ks[7], (D_HID, D_HID)), 'h2_s': jax.random.uniform(ks[8], (D_HID,), dtype=jnp.float32) * inv(D_HID), 'w3_w': _ternary(ks[9], (D_IN, D_HID)), 'w3_s': jax.random.uniform(ks[10], (D_IN,), dtype=jnp.float32) * inv(D_HID)}
    _L0_ffn_in = _L0_ffn_setup()

    def _L1_attn_setup():
        import jax, jax.numpy as jnp
        import numpy as np
        B, S, DM, H = (4, 128, 128, 16)
        D = DM // H

        def _split_heads(x):
            return x.reshape(x.shape[0], x.shape[1], H, D).transpose(0, 2, 1, 3)
        key = jax.random.key(seed)
        ks = jax.random.split(key, 16)
        sc = 0.02
        return {'hidden_states': jax.random.normal(ks[0], (B, S, DM), jnp.float32), 'wq': jax.random.normal(ks[1], (DM, DM), jnp.float32) * sc, 'bq': jax.random.normal(ks[2], (DM,), jnp.float32) * sc, 'wk': jax.random.normal(ks[3], (DM, DM), jnp.float32) * sc, 'bk': jax.random.normal(ks[4], (DM,), jnp.float32) * sc, 'wv': jax.random.normal(ks[5], (DM, DM), jnp.float32) * sc, 'bv': jax.random.normal(ks[6], (DM,), jnp.float32) * sc, 'wo': jax.random.normal(ks[7], (DM, DM), jnp.float32) * sc, 'bo': jax.random.normal(ks[8], (DM,), jnp.float32) * sc, 'wfq': jax.random.normal(ks[9], (DM, DM), jnp.float32) * sc, 'bfq': jax.random.normal(ks[10], (DM,), jnp.float32) * sc, 'wfg': jax.random.normal(ks[11], (DM, DM), jnp.float32) * sc, 'bfg': jax.random.normal(ks[12], (DM,), jnp.float32) * sc, 'up': jax.random.normal(ks[13], (H, 1, D), jnp.float32) * sc, 'uz': jax.random.normal(ks[14], (H, 1, D), jnp.float32) * sc}
    _L1_attn_in = _L1_attn_setup()

    def _L1_ffn_setup():
        import jax, jax.numpy as jnp
        import numpy as np
        ALPHA = 1.0
        key = jax.random.key(seed)
        ks = jax.random.split(key, 7)
        B, S, IN, OUT = (8, 1024, 128, 128)
        RANK, DDIM, UDIM = (4, 100, 50)
        return {'hidden_states': jax.random.normal(ks[0], (B, S, IN), dtype=jnp.float32), 'W': jax.random.normal(ks[1], (OUT, IN), dtype=jnp.float32) * 0.02, 'b': jax.random.normal(ks[2], (OUT,), dtype=jnp.float32) * 0.02, 'lora_down': jax.random.normal(ks[3], (RANK, DDIM), dtype=jnp.float32) * 0.1, 'lora_up': jax.random.normal(ks[4], (UDIM, RANK), dtype=jnp.float32) * 0.1, 'down_aux': jax.random.normal(ks[5], (DDIM, IN), dtype=jnp.float32) * 0.03, 'up_aux': jax.random.normal(ks[6], (OUT, UDIM), dtype=jnp.float32) * 0.03}
    _L1_ffn_in = _L1_ffn_setup()
    _d = {'L0_attn_x': _L0_attn_in['x'], 'L0_attn_Q_w': _L0_attn_in['Q_w'], 'L0_attn_Q_b': _L0_attn_in['Q_b'], 'L0_attn_K_w': _L0_attn_in['K_w'], 'L0_attn_K_b': _L0_attn_in['K_b'], 'L0_attn_V_w': _L0_attn_in['V_w'], 'L0_attn_V_b': _L0_attn_in['V_b'], 'L0_attn_O_w': _L0_attn_in['O_w'], 'L0_attn_O_b': _L0_attn_in['O_b'], 'L0_ffn_w1_w': _L0_ffn_in['w1_w'], 'L0_ffn_w1_s': _L0_ffn_in['w1_s'], 'L0_ffn_w2_w': _L0_ffn_in['w2_w'], 'L0_ffn_w2_s': _L0_ffn_in['w2_s'], 'L0_ffn_h1_w': _L0_ffn_in['h1_w'], 'L0_ffn_h1_s': _L0_ffn_in['h1_s'], 'L0_ffn_h2_w': _L0_ffn_in['h2_w'], 'L0_ffn_h2_s': _L0_ffn_in['h2_s'], 'L0_ffn_w3_w': _L0_ffn_in['w3_w'], 'L0_ffn_w3_s': _L0_ffn_in['w3_s'], 'L1_attn_wq': _L1_attn_in['wq'], 'L1_attn_bq': _L1_attn_in['bq'], 'L1_attn_wk': _L1_attn_in['wk'], 'L1_attn_bk': _L1_attn_in['bk'], 'L1_attn_wv': _L1_attn_in['wv'], 'L1_attn_bv': _L1_attn_in['bv'], 'L1_attn_wo': _L1_attn_in['wo'], 'L1_attn_bo': _L1_attn_in['bo'], 'L1_attn_wfq': _L1_attn_in['wfq'], 'L1_attn_bfq': _L1_attn_in['bfq'], 'L1_attn_wfg': _L1_attn_in['wfg'], 'L1_attn_bfg': _L1_attn_in['bfg'], 'L1_attn_up': _L1_attn_in['up'], 'L1_attn_uz': _L1_attn_in['uz'], 'L1_ffn_W': _L1_ffn_in['W'], 'L1_ffn_b': _L1_ffn_in['b'], 'L1_ffn_lora_down': _L1_ffn_in['lora_down'], 'L1_ffn_lora_up': _L1_ffn_in['lora_up'], 'L1_ffn_down_aux': _L1_ffn_in['down_aux'], 'L1_ffn_up_aux': _L1_ffn_in['up_aux']}
    _x0 = _d['L0_attn_x']
    _d['L0_attn_x'] = jax.random.normal(jax.random.fold_in(jax.random.key(seed), 1), (1, 2048, 128), dtype=_x0.dtype)
    del _x0
    return _d

def reference(L0_attn_x, L0_attn_Q_w, L0_attn_Q_b, L0_attn_K_w, L0_attn_K_b, L0_attn_V_w, L0_attn_V_b, L0_attn_O_w, L0_attn_O_b, L0_ffn_w1_w, L0_ffn_w1_s, L0_ffn_w2_w, L0_ffn_w2_s, L0_ffn_h1_w, L0_ffn_h1_s, L0_ffn_h2_w, L0_ffn_h2_s, L0_ffn_w3_w, L0_ffn_w3_s, L1_attn_wq, L1_attn_bq, L1_attn_wk, L1_attn_bk, L1_attn_wv, L1_attn_bv, L1_attn_wo, L1_attn_bo, L1_attn_wfq, L1_attn_bfq, L1_attn_wfg, L1_attn_bfg, L1_attn_up, L1_attn_uz, L1_ffn_W, L1_ffn_b, L1_ffn_lora_down, L1_ffn_lora_up, L1_ffn_down_aux, L1_ffn_up_aux):

    def _L0_attn_ref(x, Q_w, Q_b, K_w, K_b, V_w, V_b, O_w, O_b):
        import jax, jax.numpy as jnp
        import numpy as np
        import math
        N_HEADS, D_HEAD, D_MODEL = (16, 64, 128)
        B, S = (4, 256)
        NEG_MASK = -100000.0
        q = jnp.einsum('bpm,hmd->bphd', x, Q_w) + Q_b
        k = jnp.einsum('bpm,hmd->bphd', x, K_w) + K_b
        v = jnp.einsum('bpm,hmd->bphd', x, V_w) + V_b
        logits = jnp.einsum('bqhd,bkhd->bhqk', q, k) / math.sqrt(D_HEAD)
        s = logits.shape[-1]
        causal = jnp.triu(jnp.ones((s, s), dtype=bool), k=1)
        logits = jnp.where(causal, NEG_MASK, logits)
        scores = jax.nn.softmax(logits, axis=-1)
        attn = jnp.einsum('bhqk,bkhd->bqhd', scores, v)
        return jnp.einsum('bqhd,hdm->bqm', attn, O_w) + O_b

    def _L0_ffn_ref(x, w1_w, w1_s, w2_w, w2_s, h1_w, h1_s, h2_w, h2_s, w3_w, w3_s):
        import jax, jax.numpy as jnp
        import numpy as np
        D_IN, D_HID = (128, 512)

        def _ternary(key, shape):
            return jax.random.randint(key, shape, -1, 2).astype(jnp.float32)

        def _tlin(x, w, s):
            return jnp.einsum('bsi,oi->bso', x, w) * s
        h = jax.nn.silu(_tlin(x, w1_w, w1_s)) * _tlin(x, w2_w, w2_s)
        h = jax.nn.gelu(_tlin(h, h1_w, h1_s), approximate=False)
        h = jax.nn.gelu(_tlin(h, h2_w, h2_s), approximate=False)
        return _tlin(h, w3_w, w3_s)

    def _L1_attn_ref(hidden_states, wq, bq, wk, bk, wv, bv, wo, bo, wfq, bfq, wfg, bfg, up, uz):
        import jax, jax.numpy as jnp
        import numpy as np
        B, S, DM, H = (4, 128, 128, 16)
        D = DM // H

        def _split_heads(x):
            return x.reshape(x.shape[0], x.shape[1], H, D).transpose(0, 2, 1, 3)
        key_len = hidden_states.shape[1]
        mixed_q = hidden_states @ wq + bq
        mixed_k = hidden_states @ wk + bk
        mixed_v = hidden_states @ wv + bv
        glo = jnp.mean(mixed_q, axis=1, keepdims=True)
        c = jnp.tanh(mixed_q @ wfq + bfq + (glo @ wfg + bfg))
        c = _split_heads(c)
        p = jnp.sum(c * up[None], axis=-1)
        z = jnp.sum(c * uz[None], axis=-1)
        P = jax.nn.sigmoid(p) * key_len
        Z = jax.nn.sigmoid(z) * key_len
        j = jnp.arange(key_len, dtype=P.dtype)
        G = -(j[None, None, None, :] - P[..., None]) ** 2 * 2.0 / Z[..., None] ** 2
        q = _split_heads(mixed_q)
        k = _split_heads(mixed_k)
        v = _split_heads(mixed_v)
        scores = jnp.einsum('bhqd,bhkd->bhqk', q, k) / jnp.sqrt(jnp.float32(D))
        scores = scores + G
        probs = jax.nn.softmax(scores, axis=-1)
        ctx = jnp.einsum('bhqk,bhkd->bhqd', probs, v)
        ctx = ctx.transpose(0, 2, 1, 3).reshape(ctx.shape[0], key_len, H * D)
        return ctx @ wo + bo

    def _L1_ffn_ref(hidden_states, W, b, lora_down, lora_up, down_aux, up_aux):
        import jax, jax.numpy as jnp
        import numpy as np
        ALPHA = 1.0
        lilora_weight = up_aux @ (lora_up @ (lora_down @ down_aux))
        base = jnp.einsum('bsi,oi->bso', hidden_states, W) + b
        delta = jnp.einsum('bsi,oi->bso', hidden_states, lilora_weight)
        return base + ALPHA * delta
    x = L0_attn_x
    x = _layernorm(x + _L0_attn_ref(x, L0_attn_Q_w, L0_attn_Q_b, L0_attn_K_w, L0_attn_K_b, L0_attn_V_w, L0_attn_V_b, L0_attn_O_w, L0_attn_O_b), axis=-1)
    x = _layernorm(x + _L0_ffn_ref(x, L0_ffn_w1_w, L0_ffn_w1_s, L0_ffn_w2_w, L0_ffn_w2_s, L0_ffn_h1_w, L0_ffn_h1_s, L0_ffn_h2_w, L0_ffn_h2_s, L0_ffn_w3_w, L0_ffn_w3_s), axis=-1)
    x = _layernorm(x + _L1_attn_ref(x, L1_attn_wq, L1_attn_bq, L1_attn_wk, L1_attn_bk, L1_attn_wv, L1_attn_bv, L1_attn_wo, L1_attn_bo, L1_attn_wfq, L1_attn_bfq, L1_attn_wfg, L1_attn_bfg, L1_attn_up, L1_attn_uz), axis=-1)
    x = _layernorm(x + _L1_ffn_ref(x, L1_ffn_W, L1_ffn_b, L1_ffn_lora_down, L1_ffn_lora_up, L1_ffn_down_aux, L1_ffn_up_aux), axis=-1)
    return x

_drawn_inputs = setup_inputs


def setup_inputs(seed=0):
    import zlib

    import numpy as np

    out = dict(_drawn_inputs(seed))
    spreads = {'L0_attn_Q_b': (0.0, 0.1),
     'L0_attn_K_b': (0.0, 2.0),
     'L0_attn_V_b': (0.0, 0.1),
     'L0_attn_O_b': (0.0, 0.1)}
    factors = {'L0_ffn_w1_w': 8.0,
     'L0_ffn_w1_s': 8.0,
     'L0_ffn_w2_w': 8.0,
     'L0_ffn_w2_s': 8.0,
     'L0_ffn_h1_w': 8.0,
     'L0_ffn_h1_s': 8.0,
     'L0_ffn_h2_w': 8.0,
     'L0_ffn_h2_s': 8.0,
     'L0_ffn_w3_w': 8.0,
     'L0_ffn_w3_s': 8.0,
     'L1_attn_wq': 8.0,
     'L1_attn_bq': 24.994,
     'L1_attn_wk': 8.0,
     'L1_attn_bk': 64.0,
     'L1_attn_wv': 3.685,
     'L1_attn_bv': 8.0,
     'L1_attn_wo': 3.38,
     'L1_attn_wfq': 28.38,
     'L1_attn_bfq': 64.0,
     'L1_attn_wfg': 46.108,
     'L1_attn_bfg': 64.0,
     'L1_attn_up': 28.687,
     'L1_attn_uz': 62.584,
     'L1_ffn_b': 11.876,
     'L1_ffn_lora_down': 4.013,
     'L1_ffn_lora_up': 4.363,
     'L1_ffn_down_aux': 3.767,
     'L1_ffn_up_aux': 4.088,
     'L1_attn_bo': 4.401}
    for name, (base, spread) in spreads.items():
        noise = np.random.default_rng([zlib.crc32(name.encode()), seed]).standard_normal(out[name].shape)
        drawn = base * np.exp(spread * noise) if base else spread * noise
        out[name] = jnp.asarray(drawn.astype(out[name].dtype))
    for name, factor in factors.items():
        out[name] = (out[name] * factor).astype(out[name].dtype)
    return out
```

```python
import math
from contextlib import ExitStack

import numpy as np
import concourse.bass as bass
from concourse import mybir

F32 = mybir.dt.float32
F16 = mybir.dt.float16
BF16 = mybir.dt.bfloat16
ALU = mybir.AluOpType
ACT = mybir.ActivationFunctionType
AX = mybir.AxisListType

P = 128
S = 2048
DM = 128
NT = S // P
QC = 512
NQ = S // QC
H0, D0 = 16, 64
H1, D1 = 16, 8
HID = 512
RP = 4
NEG = -1e30
EPS = 1e-5
HEADROOM = 20.0
assert DM == P and 2 * D0 == P and H1 * D1 == DM


def norm_block(nc, tag, yt, x_sb, xt, ident, out_dram=None):
    with ExitStack() as ctx:
        def sb(name, shape, dt):
            return ctx.enter_context(nc.sbuf_tensor(f"{name}_{tag}", shape, dt))

        def sem(name):
            return ctx.enter_context(nc.semaphore(f"{name}_{tag}"))

        stats = sb("stats", [P, NT, 6], F32)
        mv = sb("mv", [P, NT, 2], F32)
        veps = sb("veps", [P, NT], F32)
        root = sb("root", [P, NT], F32)
        rstd = sb("rstd", [P, NT], F32)
        t1 = sb("t1", [P, NT], F32)
        ps_y = ctx.enter_context(nc.psum_tensor(f"ps_y_{tag}", [P, 4, 4, P], F32))
        ps_t = ctx.enter_context(nc.psum_tensor(f"ps_t_{tag}", [P, 4, QC], F32))
        s_y = sem("s_y")
        s_ve = sem("s_ve")
        s_rt = sem("s_rt")
        s_n = sem("s_n")
        s_xp = sem("s_xp")
        s_xc = sem("s_xc")
        s_dv = sem("s_dv")
        s_out = sem("s_out")
        block = ctx.enter_context(nc.Block())

        @block.tensor
        def _(pe):
            for g in range(4):
                for t in range(4):
                    tr = pe.transpose(ps_y[:, g, t, :], yt[:, (4 * g + t) * P:(4 * g + t + 1) * P], ident[:, :])
                tr.then_inc(s_y, 1)
            if out_dram is None:
                for g in range(4):
                    pe.wait_ge(s_n, 4 * g + 4)
                    for t in range(4):
                        tr = pe.transpose(ps_t[:, g, t * P:(t + 1) * P], x_sb[:, 4 * g + t, :], ident[:, :])
                    tr.then_inc(s_xp, 1)

        @block.scalar
        def _(act):
            for g in range(4):
                act.wait_ge(s_ve, g + 1)
                act.activation(root[:, 4 * g:4 * g + 4], veps[:, 4 * g:4 * g + 4], ACT.Sqrt).then_inc(s_rt, 1)
            if out_dram is None:
                for g in range(4):
                    act.wait_ge(s_xp, g + 1)
                    act.activation(xt[:, g * QC:(g + 1) * QC], ps_t[:, g, :], ACT.Copy).then_inc(s_xc, 1)
                act.wait_ge(s_xc, 4)

        @block.vector
        def _(dve):
            done = [0]

            def link(ins):
                done[0] += 1
                ins.then_inc(s_dv, 1)
                dve.wait_ge(s_dv, done[0])

            def statistics(g):
                dve.wait_ge(s_y, g + 1)
                for t in range(4):
                    ins = dve.bn_stats(stats[:, 4 * g + t, :], ps_y[:, g, t, :])
                link(ins)
                for t in range(4):
                    ins = dve.bn_aggr(mv[:, 4 * g + t, :], stats[:, 4 * g + t, :])
                link(ins)
                dve.tensor_scalar(veps[:, 4 * g:4 * g + 4], mv[:, 4 * g:4 * g + 4, 1], EPS, None, ALU.add)\
                    .then_inc(s_ve, 1)

            def apply(g):
                c = slice(4 * g, 4 * g + 4)
                dve.wait_ge(s_rt, g + 1)
                dve.wait_ge(s_ve, g + 1)
                link(dve.reciprocal(rstd[:, c], root[:, c]))
                link(dve.tensor_tensor(t1[:, c], rstd[:, c], rstd[:, c], ALU.mult))
                link(dve.tensor_tensor(t1[:, c], t1[:, c], veps[:, c], ALU.mult))
                link(dve.tensor_scalar(t1[:, c], t1[:, c], -0.5, 1.5, ALU.mult, ALU.add))
                link(dve.tensor_tensor(rstd[:, c], rstd[:, c], t1[:, c], ALU.mult))
                for t in range(4):
                    n = 4 * g + t
                    dve.tensor_scalar(x_sb[:, n, :], ps_y[:, g, t, :], mv[:, n, 0:1], rstd[:, n:n + 1],
                                      ALU.subtract, ALU.mult).then_inc(s_n, 1)

            statistics(0)
            for g in range(4):
                if g < 3:
                    statistics(g + 1)
                apply(g)

        if out_dram is not None:
            @block.sync
            def _(sp):
                for g in range(4):
                    sp.wait_ge(s_n, 4 * g + 4)
                    sp.dma_start(out_dram.rearrange("(t p) d -> p t d", p=P)[:, 4 * g:4 * g + 4, :],
                                 x_sb[:, 4 * g:4 * g + 4, :]).then_inc(s_out, 16)
                sp.wait_ge(s_out, 64)



def build(nc, a, out):
    x_dram = a["L0_attn_x"].rearrange("b s d -> (b s) d")
    out_dram = out.rearrange("b s d -> (b s) d")
    persist = ExitStack()
    x_sb = persist.enter_context(nc.sbuf_tensor("x_sb", [P, NT, DM], F32))
    xt = persist.enter_context(nc.sbuf_tensor("xt", [P, S], F32))
    yt = persist.enter_context(nc.sbuf_tensor("yt", [P, S], F32))
    ident = persist.enter_context(nc.sbuf_tensor("ident", [P, P], F32))
    with ExitStack() as ctx:
        def sb(name, shape, dt):
            return ctx.enter_context(nc.sbuf_tensor(name, shape, dt))

        def psum(name, shape, dt=F32):
            return ctx.enter_context(nc.psum_tensor(name, shape, dt))

        def sem(name):
            return ctx.enter_context(nc.semaphore(name))

        v_all = sb("v_all", [P, NT, H0 * D0], F32)
        v_head = sb("v_head", [P, 2, NT, D0], F32)
        wv = sb("wv", [P, H0, D0], F32)
        vbias = sb("vbias", [P, H0 * D0], F32)
        wqk = sb("wqk", [P, 2, 2 * D0], F32)
        wo2 = sb("wo2", [P, 2, P], F32)
        obias = sb("obias", [P, 1], F32)
        qkbias = sb("qkbias", [P, H0], F32)
        qkbias_head = sb("qkbias_head", [P, 2], F32)
        qkscale = sb("qkscale", [P, 1], F32)
        qk32 = sb("qk32", [P, 2, QC], F32)
        qk_hi = sb("qk_hi", [P, S], F16)
        qk_lo = sb("qk_lo", [P, S], F16)
        qq = sb("qq", [P, 2, S], F16)
        kk = sb("kk", [P, 2, S], F16)
        qm = sb("qm", [P, 2, S], F16)
        km = sb("km", [P, 2, S], F16)
        maxpart = sb("maxpart", [P, NT, NQ], F32)
        rowmax = sb("rowmax", [P, 4], F32)
        maxhl = sb("maxhl", [P, 2, 4], F16)
        maxrow = sb("maxrow", [8, 2, P], F16)
        probs = sb("probs", [P, RP, 2, QC], F32)
        acc = sb("acc", [P, 2, 2, QC], F32)
        accsum = sb("accsum", [P, QC], F32)
        rden = sb("rden", [P, QC], F32)
        pv_raw = sb("pv_raw", [P, QC], F32)
        pv_norm = sb("pv_norm", [P, QC], F32)
        ones = sb("ones", [P, P], F32)
        zeros = sb("zeros", [P, 1, 1], F32)
        mask = sb("mask", [P, P], BF16)
        allneg = sb("allneg", [P, P], BF16)
        identb = sb("identb", [P, P], BF16)
        identh = sb("identh", [P, P], F16)

        ps_e = psum("ps_e", [P, 2, 2, QC])
        ps_m = psum("ps_m", [P, 2, QC])
        ps_o = psum("ps_o", [P, QC])
        ps_x = psum("ps_x", [P, QC])
        ps_xh = ps_x[:, :].bitcast(F16)

        s_ld = sem("s_ld")
        s_ldx = sem("s_ldx")
        s_cst = sem("s_cst")
        s_cstv = sem("s_cstv")
        s_xt = sem("s_xt")
        s_xtc = sem("s_xtc")
        s_vp = sem("s_vp")
        s_vc = sem("s_vc")
        s_wqk = [sem(f"s_wqk{n}") for n in range(2)]
        s_wo = [sem(f"s_wo{n}") for n in range(2)]
        s_qkp = sem("s_qkp")
        s_t32 = sem("s_t32")
        s_lo = sem("s_lo")
        s_qkd = [sem(f"s_qkd{n}") for n in range(2)]
        s_mxp = sem("s_mxp")
        s_mxr = sem("s_mxr")
        s_mhl = sem("s_mhl")
        s_mc = sem("s_mc")
        s_mrd = [sem(f"s_mrd{n}") for n in range(2)]
        s_st = sem("s_st")
        s_ex = sem("s_ex")
        s_pv = sem("s_pv")
        s_ad = sem("s_ad")
        s_oc = sem("s_oc")
        s_hv = sem("s_hv")
        s_vh = sem("s_vh")
        s_xf = sem("s_xf")
        s_sb = sem("s_sb")
        s_rd = sem("s_rd")
        s_on = sem("s_on")
        s_op = sem("s_op")
        s_ac = sem("s_ac")
        s_dv = sem("s_dv")
        s_qb = sem("s_qb")
        s_mt = sem("s_mt")

        PAIRS = [(qc, kp) for qc in range(NQ) for kp in range(2 * qc + 2)]
        NP = len(PAIRS)
        LAST = [n for n, (qc, kp) in enumerate(PAIRS) if kp == 2 * qc + 1]
        CH = [(qt, c) for qt in range(NT) for c in range(qt // 4 + 1)]
        NCH = len(CH)
        GEND = [sum(4 * (g + 1) for g in range(k + 1)) for k in range(4)]
        SLOT_CH = {p: (2 * (p - 2), 2 * (p - 2) + 2) for p in range(2, 18)}
        TAIL_CH = (32, NCH)
        QK_AT = {9: 0, 12: 1, 13: 2, 15: 3}
        SB_AT = {4: 0, 8: 1, 14: 2}
        OP_AT = {6: 0, 10: 1, 16: 2}
        MT_AT = {7: 0, 11: 1, 17: 2}

        def shared_uses(do_max, do_proj):
            out = []
            for p in range(NP):
                if p in QK_AT and do_proj:
                    out.append(("qk", QK_AT[p]))
                if p in MT_AT and do_max:
                    out.append(("mt", MT_AT[p]))
                if p in SB_AT:
                    out.append(("sb", SB_AT[p]))
                if p in OP_AT:
                    out.append(("op", OP_AT[p]))
            out.append(("sb", 3))
            if do_max:
                out.append(("mt", 3))
            out.append(("op", 3))
            return out

        PRE = [("qk", c) for c in range(8)] + [("mt", g) for g in range(4)]
        FULL = shared_uses(True, True)

        def shared(h, do_max, do_proj, use):
            before = len(PRE) + len(FULL) * h if not (isinstance(h, int) and h == H0 - 1) else \
                len(PRE) + len(FULL) * (H0 - 2) + len(shared_uses(True, False))
            return before + shared_uses(do_max, do_proj).index(use)

        def diag(qc, kt):
            return kt - 4 * qc if kt >= 4 * qc else None

        def off(qc, kt):
            j = diag(qc, kt)
            return 0 if j is None or kt < 2 else P * j

        def load_wqk(eng, h, j):
            for r, name in enumerate(("L0_attn_Q_w", "L0_attn_K_w")):
                eng.dma_start(wqk[:, j, D0 * r:D0 * r + D0], a[name][bass.ds(h, 1)].rearrange("a m d -> m (a d)"))\
                    .then_inc(s_wqk[j], 16)

        def load_wo(eng, h, j):
            for r in range(2):
                eng.dma_start(wo2[D0 * r:D0 * r + D0, j, :],
                              a["L0_attn_O_w"][bass.ds(h, 1)].rearrange("a d m -> d (a m)")).then_inc(s_wo[j], 16)

        block = ctx.enter_context(nc.Block())

        @block.sync
        def _(sp):
            sp.dma_start(x_sb[:, :, :], x_dram.rearrange("(t p) d -> p t d", p=P)).then_inc(s_ldx, 16)
            sp.dma_start(wv[:, :, :], a["L0_attn_V_w"].rearrange("h m d -> m h d")).then_inc(s_ld, 16)

            for h in range(2):
                load_wqk(sp, h, h)
            load_wo(sp, 0, 0)
            vb = a["L0_attn_V_b"].rearrange("h d -> (h d)").rearrange("(a n) -> a n", a=1)
            sp.dma_start(vbias[:, :], vb.to_broadcast([P, H0 * D0])).then_inc(s_ld, 16)
            with nc.allow_non_contiguous_dma(reason="small bias columns"):
                sp.dma_start(qkbias[0:D0, :], a["L0_attn_Q_b"].rearrange("h d -> d h")).then_inc(s_ld, 16)
                sp.dma_start(qkbias[D0:P, :], a["L0_attn_K_b"].rearrange("h d -> d h")).then_inc(s_ld, 16)
                sp.dma_start(obias[:, :], a["L0_attn_O_b"].rearrange("(m a) -> m a", a=1)).then_inc(s_ld, 16)

            def place_operands(h, j, read=None):
                made = 4 * h + 4
                if read is not None and not isinstance(read, int):
                    made, read = sp.snap(made), sp.snap(read)
                sp.wait_ge(s_lo, made)
                if read is not None:
                    sp.wait_ge(s_st, read)
                for dst, src in ((qq[0:D0, j], qk_hi[0:D0]), (qq[D0:P, j], qk_lo[0:D0]), (kk[0:D0, j], qk_hi[D0:P]),
                                 (kk[D0:P, j], qk_hi[D0:P]), (qm[0:D0, j], qk_hi[0:D0]), (km[0:D0, j], qk_lo[D0:P])):
                    sp.dma_start(dst, src).then_inc(s_qkd[j], 16)

            def place_max(h, j, g):
                sp.wait_ge(s_mc, 4 * h + g + 1)
                for r in range(2):
                    sp.dma_start(qm[D0 + r:D0 + r + 1, j, g * QC:(g + 1) * QC].rearrange("a (t q) -> a t q", q=P),
                                 maxrow[4 * r:4 * r + 4, g % 2, :])\
                        .then_inc(s_mrd[g % 2], 16)

            place_operands(0, 0)
            place_operands(1, 1)
            for g in range(4):
                place_max(0, 0, g)

            def step(h, j, do_max, do_proj):
                if do_max:
                    for g in range(3):
                        place_max(h + 1, 1 - j, g)
                if do_proj:
                    place_operands(h + 2, j, NP * h + NP)
                if do_max:
                    place_max(h + 1, 1 - j, 3)

            with sp.Fori(0, H0 - 3, 2) as i:
                step(i, 0, True, True)
                step(i + 1, 1, True, True)
            step(H0 - 2, 0, True, False)
            step(H0 - 1, 1, False, False)

        @block.gpsimd
        def _(pool):
            pool.memset(ident[:, :], 0.0).then_inc(s_cst, 1)
            pool.memset(mask[:, :], 0.0).then_inc(s_cst, 1)
            pool.memset(allneg[:, :], NEG).then_inc(s_cst, 1)
            pool.memset(ones[:, :], 1.0).then_inc(s_cst, 1)
            pool.memset(zeros[:, :, :], 0.0).then_inc(s_cst, 1)
            pool.wait_ge(s_cst, 5)
            pool.affine_select(out=ident[:, :], in_=ident[:, :], compare_op=ALU.not_equal, fill=1.0,
                               base=0, pattern=[[-1, P]], channel_multiplier=1).then_inc(s_cst, 1)
            pool.affine_select(out=mask[:, :], in_=mask[:, :], compare_op=ALU.is_ge, fill=NEG,
                               base=0, pattern=[[-1, P]], channel_multiplier=1).then_inc(s_cst, 1)
            pool.sem_inc(s_ad, RP)

            def step(h):
                for p, (qc, kp) in enumerate(PAIRS):
                    pr = probs[:, p % RP]
                    pool.wait_ge(s_ex, NP * h + p + 3)
                    if kp == 0:
                        pool.wait_ge(s_hv, 4 * h + qc + 1)
                        pool.tensor_tensor(acc[:, qc % 2], pr, zeros[:, :, :].to_broadcast([P, 2, QC]), ALU.add)\
                            .then_inc(s_ad, 1)
                        continue
                    pool.wait_ge(s_ad, NP * h + p + RP)
                    if diag(qc, 2 * kp) is None:
                        pool.tensor_tensor(acc[:, qc % 2], acc[:, qc % 2], pr, ALU.add).then_inc(s_ad, 1)
                    else:
                        for u in range(2):
                            o = off(qc, 2 * kp + u)
                            add = pool.tensor_tensor(acc[:, qc % 2, u, o:], acc[:, qc % 2, u, o:], pr[:, u, o:], ALU.add)
                        add.then_inc(s_ad, 1)

            with pool.Fori(0, H0 - 3, 2) as i:
                step(i)
                step(i + 1)
            step(H0 - 2)
            step(H0 - 1)

        @block.scalar
        def _(act):
            act.wait_ge(s_cstv, 5)
            act.sem_inc(s_ex, 2)
            act.sem_inc(s_oc, 1)

            def cast(h, j, c):
                act.wait_ge(s_qkp, 4 * h + c + 1)
                if not isinstance(h, int) or 4 * h + c >= 2:
                    act.wait_ge(s_lo, 4 * h + c - 1)
                if not isinstance(h, int) or h >= 1:
                    act.wait_ge(s_qkd[1 - j], 48 * (h + j))
                act.wait_ge(s_qb, h + 1)
                act.activation(qk32[:, c % 2, :], ps_x[:, :], ACT.Identity, bias=qkbias_head[:, j:j + 1],
                               scale=qkscale[:, 0:1])
                act.activation(qk_hi[:, c * QC:(c + 1) * QC], ps_x[:, :], ACT.Identity,
                               bias=qkbias_head[:, j:j + 1], scale=qkscale[:, 0:1]).then_inc(s_t32, 1)

            def exps(h, p):
                qc, kp = PAIRS[p]
                act.wait_ge(s_st, NP * h + p + 1)
                act.wait_ge(s_pv, NP * h + p + 1)
                act.wait_ge(s_ad, NP * h + p + 1)
                if diag(qc, 2 * kp) is None:
                    act.activation(probs[:, p % RP], ps_e[:, p % 2], ACT.Exp).then_inc(s_ex, 1)
                else:
                    for u in range(2):
                        o = off(qc, 2 * kp + u)
                        e = act.activation(probs[:, p % RP, u, o:], ps_e[:, p % 2, u, o:], ACT.Exp)
                    e.then_inc(s_ex, 1)

            def copy_pv(h, qc):
                act.wait_ge(s_pv, NP * h + LAST[qc] + 1 + RP)
                act.wait_ge(s_on, 4 * h + qc + 1)
                act.activation(pv_raw[:, :], ps_o[:, :], ACT.Copy).then_inc(s_oc, 1)

            for h in range(2):
                for c in range(4):
                    cast(h, h, c)

            def step(h, j, do_max, do_proj):
                for p in range(NP):
                    exps(h, p)
                    if p == 4:
                        if do_proj:
                            load_wqk(act, h + 2, j)
                        if do_max:
                            load_wo(act, h + 1, 1 - j)
                    if p in QK_AT and do_proj:
                        cast(h + 2, j, QK_AT[p])
                    if p - 1 in LAST:
                        copy_pv(h, LAST.index(p - 1))
                copy_pv(h, 3)

            with act.Fori(0, H0 - 3, 2) as i:
                step(i, 0, True, True)
                step(i + 1, 1, True, True)
            step(H0 - 2, 0, True, False)
            step(H0 - 1, 1, False, False)

        @block.tensor
        def _(pe):
            pe.sem_inc(s_pv, RP)
            pe.sem_inc(s_sb, 1)
            pe.sem_inc(s_op, 1)
            pe.wait_ge(s_cst, 7)
            pe.wait_ge(s_ldx, 16)
            for n in range(4):
                if n >= 2:
                    pe.wait_ge(s_xtc, n - 1)
                for t in range(4):
                    tr = pe.transpose(ps_m[:, n % 2, t * P:(t + 1) * P], x_sb[:, 4 * n + t, :], ident[:, :])
                tr.then_inc(s_xt, 1)
            pe.wait_ge(s_ld, 80)
            pe.wait_ge(s_xtc, 4)
            for t in range(NT):
                for c in range(2):
                    n = 2 * t + c
                    if n >= 4:
                        pe.wait_ge(s_vc, n - 3)
                    pe.matmul(ps_e[:, (n % 4) // 2, n % 2], xt[:, t * P:(t + 1) * P],
                              wv[:, 8 * c:8 * c + 8, :].rearrange("m h d -> m (h d)"),
                              start=True, stop=True).then_inc(s_vp, 1)

            def proj(h, j, c, before):
                pe.wait_ge(s_xf, before + 1)
                if c == 0:
                    pe.wait_ge(s_wqk[j], 16 * (h - j) + 32)
                pe.matmul(ps_x[:, :], wqk[:, j, :], xt[:, c * QC:(c + 1) * QC], start=True, stop=True)\
                    .then_inc(s_qkp, 1)

            def max_chunk(h, j, n):
                qt, c = CH[n]
                if n == 0:
                    pe.wait_ge(s_qkd[j], 48 * (h - j) + 96)
                pe.wait_ge(s_mxr, NCH * h + n + 1)
                end = c == qt // 4
                w = P * (qt % 4 + 1) if end else QC
                mm = pe.matmul(ps_m[:, n % 2, 0:w], qq[:, j, qt * P:(qt + 1) * P], kk[:, j, c * QC:c * QC + w],
                               start=True, stop=not end)
                if end:
                    mm = pe.matmul(ps_m[:, n % 2, w - P:w], identb[:, :], mask[:, :], start=False, stop=True)
                mm.then_inc(s_mxp, 1)

            def max_transpose(h, g, before):
                pe.wait_ge(s_mhl, 4 * h + g + 1)
                pe.wait_ge(s_xf, before + 1)
                pe.transpose(ps_xh[0:8, 0:P], maxhl[:, :, :].rearrange("p r t -> p (r t)"), identh[:, :])\
                    .then_inc(s_mt, 1)

            def scores(h, j, p):
                qc, kp = PAIRS[p]
                if kp == 0:
                    pe.wait_ge(s_mrd[qc % 2], 64 * h + 32 * (qc // 2 + 1))
                pe.wait_ge(s_ex, NP * h + p + 1)
                for u in range(2):
                    kt = 2 * kp + u
                    o = off(qc, kt)
                    out = ps_e[:, p % 2, u]
                    keys = slice(kt * P, (kt + 1) * P)
                    queries = slice(qc * QC + o, (qc + 1) * QC)
                    jd = diag(qc, kt)
                    pe.matmul(out[:, o:], kk[:, j, keys], qq[:, j, queries], start=True, stop=False)
                    mm = pe.matmul(out[:, o:], km[0:D0 + 2, j, keys], qm[0:D0 + 2, j, queries],
                                   start=False, stop=jd is None)
                    if jd is not None:
                        for b in range(o // P, jd):
                            pe.matmul(out[:, b * P:(b + 1) * P], allneg[:, :], identb[:, :], start=False, stop=False)
                        mm = pe.matmul(out[:, jd * P:(jd + 1) * P], mask[:, :], identb[:, :], start=False, stop=True)
                mm.then_inc(s_st, 1)

            def pv(h, j, p):
                qc, kp = PAIRS[p]
                pe.wait_ge(s_ex, NP * h + p + 3)
                if p == 0:
                    pe.wait_ge(s_vh, h + 1)
                if kp == 0:
                    pe.wait_ge(s_oc, 4 * h + qc + 1)
                for u in range(2):
                    kt = 2 * kp + u
                    o = off(qc, kt)
                    mm = pe.matmul(ps_o[D0 * u:D0 * u + D0, o:], v_head[:, j, kt, :], probs[:, p % RP, u, o:],
                                   start=kp == 0, stop=p in LAST, skip_group_check=True)
                mm.then_inc(s_pv, 1)

            def spread_sums(h, qc, before):
                pe.wait_ge(s_hv, 4 * h + qc + 3)
                pe.wait_ge(s_xf, before + 1)
                pe.matmul(ps_x[:, :], ones[:, :], accsum[:, :], start=True, stop=True).then_inc(s_sb, 1)

            def out_product(h, j, qc, before):
                if qc == 0:
                    pe.wait_ge(s_wo[j], 16 * (h - j) + 32)
                pe.wait_ge(s_on, 4 * h + qc + 2)
                pe.wait_ge(s_xf, before + 1)
                pe.matmul(ps_x[:, :], wo2[:, j, :], pv_norm[:, :], start=True, stop=True).then_inc(s_op, 1)

            pe.wait_ge(s_cstv, 5)
            for h in range(2):
                for c in range(4):
                    proj(h, h, c, 4 * h + c)
            g = 0
            for n in range(NCH):
                max_chunk(0, 0, n)
                if n + 1 == GEND[g]:
                    max_transpose(0, g, 8 + g)
                    g += 1

            def step(h, j, do_max, do_proj):
                def before(*use):
                    return shared(h, do_max, do_proj, use)

                for p in range(NP):
                    scores(h, j, p)
                    if p in QK_AT and do_proj:
                        proj(h + 2, j, QK_AT[p], before("qk", QK_AT[p]))
                    if p in SLOT_CH and do_max:
                        for n in range(*SLOT_CH[p]):
                            max_chunk(h + 1, 1 - j, n)
                    if p in MT_AT and do_max:
                        max_transpose(h + 1, MT_AT[p], before("mt", MT_AT[p]))
                    if p in SB_AT:
                        spread_sums(h, SB_AT[p], before("sb", SB_AT[p]))
                    if p in OP_AT:
                        out_product(h, j, OP_AT[p], before("op", OP_AT[p]))
                    if p >= 1:
                        pv(h, j, p - 1)
                if do_max:
                    for n in range(*TAIL_CH):
                        max_chunk(h + 1, 1 - j, n)
                pv(h, j, NP - 1)
                spread_sums(h, 3, before("sb", 3))
                if do_max:
                    max_transpose(h + 1, 3, before("mt", 3))
                out_product(h, j, 3, before("op", 3))

            with pe.Fori(0, H0 - 3, 2) as i:
                step(i, 0, True, True)
                step(i + 1, 1, True, True)
            step(H0 - 2, 0, True, False)
            step(H0 - 1, 1, False, False)

        @block.vector
        def _(dve):
            dve.memset(qkscale[0:D0, :], 1.0 / math.sqrt(D0)).then_inc(s_dv, 1)
            dve.memset(qkscale[D0:P, :], 1.0).then_inc(s_dv, 1)
            dve.wait_ge(s_dv, 2)
            dve.wait_ge(s_ld, 80)
            dve.tensor_scalar(qkbias[:, :], qkbias[:, :], qkscale[:, 0:1], None, ALU.mult).then_inc(s_cstv, 1)
            dve.wait_ge(s_cstv, 1)
            for h in range(2):
                dve.tensor_copy(qkbias_head[:, h:h + 1], qkbias[:, h:h + 1]).then_inc(s_qb, 1)
            dve.wait_ge(s_cst, 7)
            dve.tensor_copy(identb[:, :], ident[:, :]).then_inc(s_cstv, 1)
            dve.tensor_copy(identh[:, :], ident[:, :]).then_inc(s_cstv, 1)
            dve.memset(km[D0:D0 + 2, :, :], -1.0).then_inc(s_cstv, 1)
            for n in range(4):
                dve.wait_ge(s_xt, n + 1)
                dve.tensor_copy(xt[:, n * QC:(n + 1) * QC], ps_m[:, n % 2]).then_inc(s_xtc, 1)
            dve.sem_inc(s_mxr, 2)
            dve.sem_inc(s_hv, 2)
            dve.sem_inc(s_on, 1)
            dve.sem_inc(s_xf, 1)
            dve.wait_ge(s_xtc, 4)
            dve.tensor_scalar(yt[:, :], xt[:, :], obias[:, 0:1], None, ALU.add).then_inc(s_cstv, 1)
            for n in range(2 * NT):
                t, c = n // 2, n % 2
                dve.wait_ge(s_vp, n + 1)
                dve.tensor_tensor(v_all[:, t, c * QC:(c + 1) * QC], ps_e[:, (n % 4) // 2, n % 2],
                                  vbias[:, c * QC:(c + 1) * QC], ALU.add).then_inc(s_vc, 1)
            dve.wait_ge(s_vc, 2 * NT)
            dve.tensor_copy(v_head[:, 0], v_all[:, :, 0:D0]).then_inc(s_vh, 1)

            def low(h, c):
                dve.wait_ge(s_t32, 4 * h + c + 1)
                dve.sem_inc(s_xf, 1)
                cols = slice(c * QC, (c + 1) * QC)
                dve.tensor_tensor(qk_lo[:, cols], qk32[:, c % 2, :], qk_hi[:, cols], ALU.subtract).then_inc(s_lo, 1)

            def take_max(h, n):
                qt, c = CH[n]
                w = P * (qt % 4 + 1) if c == qt // 4 else QC
                dve.wait_ge(s_mxp, NCH * h + n + 1)
                dve.reduce_max(maxpart[:, qt, c:c + 1], ps_m[:, n % 2, 0:w], AX.X).then_inc(s_mxr, 1)

            def split_max(h, g):
                dve.wait_ge(s_mxr, NCH * h + GEND[g] + 2)
                dve.wait_ge(s_mt, 4 * h + g)
                dve.reduce_max(rowmax[:, :], maxpart[:, 4 * g:4 * g + 4, 0:g + 1], AX.X).then_inc(s_dv, 1)
                dve.wait_ge(s_dv, 8 * h + 2 * g + 3)
                dve.tensor_copy(maxhl[:, 0, :], rowmax[:, :]).then_inc(s_dv, 1)
                dve.wait_ge(s_dv, 8 * h + 2 * g + 4)
                dve.tensor_tensor(maxhl[:, 1, :], rowmax[:, :], maxhl[:, 0, :], ALU.subtract).then_inc(s_mhl, 1)

            def max_out(h, g):
                dve.wait_ge(s_mt, 4 * h + g + 1)
                if not isinstance(h, int) or 4 * h + g >= 2:
                    dve.wait_ge(s_mrd[g % 2], 64 * h + 32 * (g // 2))
                dve.tensor_copy(maxrow[:, g % 2, :], ps_xh[0:8, 0:P]).then_inc(s_mc, 1)
                dve.wait_ge(s_mc, 4 * h + g + 1)
                dve.sem_inc(s_xf, 1)

            def add_halves(h, qc):
                dve.wait_ge(s_ad, NP * h + LAST[qc] + 1 + RP)
                dve.wait_ge(s_sb, 4 * h + qc + 1)
                dve.tensor_tensor(accsum[:, :], acc[:, qc % 2, 0], acc[:, qc % 2, 1], ALU.add).then_inc(s_hv, 1)

            def normalise(h, qc):
                dve.wait_ge(s_sb, 4 * h + qc + 2)
                dve.reciprocal(rden[:, :], ps_x[:, :]).then_inc(s_rd, 1)
                dve.wait_ge(s_rd, 4 * h + qc + 1)
                dve.sem_inc(s_xf, 1)
                dve.wait_ge(s_oc, 4 * h + qc + 2)
                dve.wait_ge(s_op, 4 * h + qc + 1)
                dve.tensor_tensor(pv_norm[:, :], pv_raw[:, :], rden[:, :], ALU.mult).then_inc(s_on, 1)

            def add_out(h, qc):
                cols = slice(qc * QC, (qc + 1) * QC)
                dve.wait_ge(s_op, 4 * h + qc + 2)
                dve.tensor_tensor(yt[:, cols], yt[:, cols], ps_x[:, :], ALU.add).then_inc(s_ac, 1)
                dve.wait_ge(s_ac, 4 * h + qc + 1)
                dve.sem_inc(s_xf, 1)

            for h in range(2):
                for c in range(4):
                    low(h, c)
            g = 0
            for n in range(NCH):
                take_max(0, n)
                if n + 1 == GEND[g]:
                    split_max(0, g)
                    max_out(0, g)
                    g += 1

            def step(h, j, do_max, do_proj):
                if do_proj:
                    dve.wait_ge(s_t32, 4 * h + 4)
                    dve.tensor_copy(qkbias_head[:, j:j + 1], qkbias[:, bass.ds(h + 2, 1)]).then_inc(s_qb, 1)
                for p in range(NP):
                    if p - 1 in SB_AT:
                        normalise(h, SB_AT[p - 1])
                    if p - 1 in OP_AT:
                        add_out(h, OP_AT[p - 1])
                    if p - 1 in MT_AT and do_max:
                        max_out(h + 1, MT_AT[p - 1])
                    if p - 1 in QK_AT and do_proj:
                        low(h + 2, QK_AT[p - 1])
                    if p in SLOT_CH and do_max:
                        for n in range(*SLOT_CH[p]):
                            take_max(h + 1, n)
                    if p + 1 in MT_AT and do_max:
                        split_max(h + 1, MT_AT[p + 1])
                    if p + 1 in SB_AT:
                        add_halves(h, SB_AT[p + 1])
                    if p == 5 and do_max:
                        dve.wait_ge(s_pv, NP * h + RP)
                        dve.tensor_copy(v_head[:, 1 - j], v_all[:, :, bass.ds((h + 1) * D0, D0)]).then_inc(s_vh, 1)
                if do_max:
                    for n in range(*TAIL_CH):
                        take_max(h + 1, n)
                    split_max(h + 1, 3)
                add_halves(h, 3)
                normalise(h, 3)
                if do_max:
                    max_out(h + 1, 3)
                add_out(h, 3)

            with dve.Fori(0, H0 - 3, 2) as i:
                step(i, 0, True, True)
                step(i + 1, 1, True, True)
            step(H0 - 2, 0, True, False)
            step(H0 - 1, 1, False, False)
    norm_block(nc, "n0", yt, x_sb, xt, ident)

    with ExitStack() as ctx:
        def sb(name, shape, dt):
            return ctx.enter_context(nc.sbuf_tensor(name, shape, dt))

        def sem(name):
            return ctx.enter_context(nc.semaphore(name))

        NH = HID // P
        LAYERS = (("w1", NH, 1), ("w2", NH, 1), ("h1", NH, NH), ("h2", NH, NH), ("w3", 1, NH))
        raw = {n: sb(f"raw_{n}", [P, o, i * P], F32) for n, o, i in LAYERS}
        wt = {n: sb(f"wt_{n}", [P, i, o * P], F32) for n, o, i in LAYERS}
        sc = {n: sb(f"sc_{n}", [P, o], F32) for n, o, i in LAYERS}
        act_a = sb("act_a", [P, NH, S], F32)
        act_b = sb("act_b", [P, NH, S], F32)
        gate = sb("gate", [P, 4, QC], F32)
        ps = [ctx.enter_context(nc.psum_tensor(f"ps_f{n}", [P, QC], F32)) for n in range(8)]

        s_w = {n: sem(f"s_w_{n}") for n, _, _ in LAYERS}
        s_tp = sem("s_tp")
        s_tc = sem("s_tc")
        s_gp = sem("s_gp")
        s_up = sem("s_up")
        s_ga = sem("s_ga")
        s_gu = sem("s_gu")
        s_hp = sem("s_hp")
        s_ha = sem("s_ha")
        s_op = sem("s_op3")
        s_oy = sem("s_oy3")

        BLOCKS = [(n, o, i) for n, no, ni in LAYERS for o in range(no) for i in range(ni)]
        GROUPS = [BLOCKS[b:b + 4] for b in range(0, len(BLOCKS), 4)]
        block = ctx.enter_context(nc.Block())

        @block.sync
        def _(sp):
            with nc.allow_non_contiguous_dma(reason="small scale columns"):
                for n, no, ni in LAYERS:
                    sp.dma_start(raw[n][:, :, :], a[f"L0_ffn_{n}_w"].rearrange("(t p) i -> p t i", p=P))\
                        .then_inc(s_w[n], 16)
                    sp.dma_start(sc[n][:, :], a[f"L0_ffn_{n}_s"].rearrange("(t p) -> p t", p=P)).then_inc(s_w[n], 16)

        @block.tensor
        def _(pe):
            seen = set()
            for g, group in enumerate(GROUPS):
                if g >= 2:
                    pe.wait_ge(s_tc, g - 1)
                for b, (n, o, i) in enumerate(group):
                    if n not in seen:
                        pe.wait_ge(s_w[n], 32)
                        seen.add(n)
                    tr = pe.transpose(ps[g % 2][:, b * P:(b + 1) * P], raw[n][:, o, i * P:(i + 1) * P], ident[:, :])
                tr.then_inc(s_tp, 1)
            pe.wait_ge(s_tc, len(GROUPS))
            for n in range(NQ * NH):
                c, o = divmod(n, NH)
                if n >= 4:
                    pe.wait_ge(s_gu, n - 3)
                cols = slice(c * QC, (c + 1) * QC)
                pe.matmul(ps[n % 4][:, :], wt["w1"][:, 0, o * P:(o + 1) * P], xt[:, cols], start=True, stop=True)\
                    .then_inc(s_gp, 1)
                pe.matmul(ps[4 + n % 4][:, :], wt["w2"][:, 0, o * P:(o + 1) * P], xt[:, cols], start=True, stop=True)\
                    .then_inc(s_up, 1)
            pe.wait_ge(s_gu, NQ * NH)

            def hidden(name, src, k):
                for n in range(NQ * NH):
                    c, o = divmod(n, NH)
                    m = NQ * NH * k + n
                    if k == 1:
                        pe.wait_ge(s_ha, NH * (c + 1))
                    if m >= 8:
                        pe.wait_ge(s_ha, m - 7)
                    for i in range(NH):
                        mm = pe.matmul(ps[m % 8][:, :], wt[name][:, i, o * P:(o + 1) * P],
                                       src[:, i, c * QC:(c + 1) * QC], start=i == 0, stop=i == NH - 1)
                    mm.then_inc(s_hp, 1)

            hidden("h1", act_a, 0)
            hidden("h2", act_b, 1)
            for c in range(NQ):
                pe.wait_ge(s_ha, max(NQ * NH + NH * (c + 1), 2 * NQ * NH - 7 + c))
                for i in range(NH):
                    mm = pe.matmul(ps[c][:, :], wt["w3"][:, i, :], act_a[:, i, c * QC:(c + 1) * QC],
                                   start=i == 0, stop=i == NH - 1)
                mm.then_inc(s_op, 1)

        @block.scalar
        def _(act):
            act.wait_ge(s_w["w1"], 32)
            for n in range(NQ * NH):
                act.wait_ge(s_gp, n + 1)
                if n >= 4:
                    act.wait_ge(s_gu, n - 3)
                act.activation(gate[:, n % 4, :], ps[n % 4][:, :], ACT.Silu, scale=sc["w1"][:, n % NH:n % NH + 1])\
                    .then_inc(s_ga, 1)
            for k, (name, dst) in enumerate((("h1", act_b), ("h2", act_a))):
                act.wait_ge(s_w[name], 32)
                for n in range(NQ * NH):
                    c, o = divmod(n, NH)
                    m = NQ * NH * k + n
                    act.wait_ge(s_hp, m + 1)
                    if k == 1 and o == 0:
                        act.wait_ge(s_hp, NH * (c + 1))
                    act.activation(dst[:, o, c * QC:(c + 1) * QC], ps[m % 8][:, :], ACT.Gelu,
                                   scale=sc[name][:, o:o + 1]).then_inc(s_ha, 1)

        @block.vector
        def _(dve):
            for g, group in enumerate(GROUPS):
                dve.wait_ge(s_tp, g + 1)
                for b, (n, o, i) in enumerate(group):
                    ins = dve.tensor_copy(wt[n][:, i, o * P:(o + 1) * P], ps[g % 2][:, b * P:(b + 1) * P])
                ins.then_inc(s_tc, 1)
            dve.wait_ge(s_w["w2"], 32)
            dve.wait_ge(s_w["w3"], 32)
            for n in range(NQ * NH):
                c, o = divmod(n, NH)
                dve.wait_ge(s_up, n + 1)
                dve.wait_ge(s_ga, n + 1)
                dve.scalar_tensor_tensor(act_a[:, o, c * QC:(c + 1) * QC], ps[4 + n % 4][:, :],
                                         sc["w2"][:, o:o + 1], gate[:, n % 4, :], ALU.mult, ALU.mult).then_inc(s_gu, 1)
            for c in range(NQ):
                dve.wait_ge(s_op, c + 1)
                cols = slice(c * QC, (c + 1) * QC)
                dve.scalar_tensor_tensor(yt[:, cols], ps[c][:, :], sc["w3"][:, 0:1], xt[:, cols],
                                         ALU.mult, ALU.add).then_inc(s_oy, 1)
            dve.wait_ge(s_oy, NQ)

    norm_block(nc, "n1", yt, x_sb, xt, ident)

    NC = 4
    KB = S // NC
    R_A, R_W1, R_W0, R_M, R_END = 9 * D1, 9 * D1 + 6, 9 * D1 + 9, 9 * D1 + 12, 9 * D1 + 14
    GR = R_M - R_A
    CH1 = NC * H1
    qd = nc.dram_tensor("q_rows", (H1, R_A, S), BF16, kind="Internal").ap()
    kd = nc.dram_tensor("k_rows", (H1, R_A, S), BF16, kind="Internal").ap()
    gd = nc.dram_tensor("g_rows", (H1, GR, NC, S), BF16, kind="Internal").ap()

    l1 = ExitStack()
    v1 = l1.enter_context(nc.sbuf_tensor("v1", [P, NT, DM], F32))
    krows = l1.enter_context(nc.sbuf_tensor("krows", [P, 2, S], BF16))

    with ExitStack() as ctx:
        def sb(name, shape, dt):
            return ctx.enter_context(nc.sbuf_tensor(name, shape, dt))

        def sem(name):
            return ctx.enter_context(nc.semaphore(name))

        w1 = {n: sb(f"l1_{n}", [P, DM], F32) for n in ("wq", "wk", "wv", "wfq", "wfg")}
        col = {n: sb(f"l1_{n}", [P, 1], F32) for n in ("bq", "bk", "bfq", "bfg", "up", "uz")}
        bv = sb("l1_bv", [P, DM], F32)
        mq = sb("mq", [P, S], F32)
        mk = sb("mk", [P, S], F32)
        qs = yt
        rest = x_sb[:, :, :].rearrange("p t d -> p (t d)")
        parts = {n: sb(f"parts_{n}", [P, 3, S], BF16) for n in "qk"}
        gparts = {n: sb(f"parts_{n}", [CH1, 3, S], BF16) for n in ("a", "w1", "w0")}
        cgate = sb("cgate", [P, S], F32)
        blk = sb("blk", [P, NC, H1], F32)
        ublk = sb("ublk", [P, NC, H1], F32)
        zblk = sb("zblk", [P, NC, H1], F32)
        sp_ = sb("sig_p", [CH1, S], F32)
        sz = sb("sig_z", [CH1, S], F32)
        na = sb("na", [CH1, S], F32)
        uu = sb("uu", [CH1, S], F32)
        f1 = sb("f1", [CH1, S], F32)
        glo = sb("glo", [P, 1], F32)
        cbias = sb("cbias", [P, 1], F32)
        centre_row = sb("centre_row", [1, CH1], F32)
        centre = sb("centre", [CH1, 1], F32)
        dj = sb("dj", [1, S], F32)
        dj2 = sb("dj2", [1, S], F32)
        crow = sb("crow", [1, 5, S], BF16)
        ps = [ctx.enter_context(nc.psum_tensor(f"ps_p{n}", [P, QC], F32)) for n in range(8)]

        s_w = sem("s_w")
        s_i = sem("s_i")
        s_ctr = sem("s_ctr")
        s_qp = sem("s_qp")
        s_qa = sem("s_qa")
        s_va = sem("s_va")
        s_bl = sem("s_bl")
        s_gl = sem("s_gl")
        s_gp = sem("s_gp")
        s_cb = sem("s_cb")
        s_cp = sem("s_cp")
        s_ca = sem("s_ca")
        s_pp = sem("s_pp")
        s_pa = sem("s_pa")
        s_pt = sem("s_pt")
        s_cr = sem("s_cr")
        s_dr = sem("s_dr")
        s_dv = sem("s_dv")
        block = ctx.enter_context(nc.Block())

        @block.sync
        def _(sp):
            n_w = 0
            for n in ("wq", "wk", "wv", "wfq", "wfg"):
                sp.dma_start(w1[n][:, :], a[f"L1_attn_{n}"]).then_inc(s_w, 16)
                n_w += 1
            with nc.allow_non_contiguous_dma(reason="small columns"):
                for n in ("bq", "bk", "bfq", "bfg"):
                    sp.dma_start(col[n][:, :], a[f"L1_attn_{n}"].rearrange("(m a) -> m a", a=1)).then_inc(s_w, 16)
                    n_w += 1
                for n in ("up", "uz"):
                    sp.dma_start(col[n][:, :], a[f"L1_attn_{n}"].rearrange("h a d -> (h d) a")).then_inc(s_w, 16)
                    n_w += 1
            sp.dma_start(bv[:, :], a["L1_attn_bv"].rearrange("(a n) -> a n", a=1).to_broadcast([P, DM]))\
                .then_inc(s_w, 16)
            assert n_w + 1 == 12
            sp.wait_ge(s_i, 4)
            with nc.allow_non_contiguous_dma(reason="a small row into a column"):
                sp.dma_start(centre[:, :], centre_row[0:1, :]).then_inc(s_ctr, 16)
            sp.wait_ge(s_cr, 5)
            n_d = 0
            for j in range(2):
                for r in range(R_END - R_A):
                    src = r % 2 if r < 6 else 2 if r < 9 else 3 if r < 12 else 4
                    sp.dma_start(krows[R_A + r:R_A + r + 1, j, :], crow[0:1, src, :]).then_inc(s_dr, 16)
                    n_d += 1
            for m, (n, dst) in enumerate((("q", qd), ("k", kd))):
                sp.wait_ge(s_pt, m + 1)
                for i in range(3):
                    for jj in range(3):
                        row = D1 * (3 * i + jj)
                        sp.dma_start(dst[:, row:row + D1, :], parts[n][:, i if n == "q" else jj, :]).then_inc(s_dr, 16)
                        n_d += 1
            for m, (n, row, rep) in enumerate((("a", 0, 2), ("w1", 6, 1), ("w0", 9, 1))):
                sp.wait_ge(s_pt, 3 + m)
                for i in range(3):
                    for r in range(rep):
                        sp.dma_start(gd[:, row + rep * i + r].rearrange("h c s -> c h s"), gparts[n][:, i, :])\
                            .then_inc(s_dr, 16)
                        n_d += 1
            sp.wait_ge(s_dr, 16 * n_d)

        @block.gpsimd
        def _(pool):
            pool.memset(blk[:, :, :], 1.0).then_inc(s_i, 1)
            pool.iota(centre_row[:, :], pattern=[[KB, NC], [0, H1]], base=KB // 2, channel_multiplier=0,
                      allow_small_or_imprecise_dtypes=True).then_inc(s_i, 1)
            pool.iota(dj[:, :], pattern=[[0, NC], [1, KB]], base=-(KB // 2), channel_multiplier=0,
                      allow_small_or_imprecise_dtypes=True).then_inc(s_i, 1)
            pool.wait_ge(s_i, 3)
            pool.affine_select(out=blk[:, :, :], in_=blk[:, :, :], compare_op=ALU.is_ge, fill=0.0,
                               base=0, pattern=[[0, NC], [-D1, H1]], channel_multiplier=1).then_inc(s_i, 1)
            pool.wait_ge(s_i, 4)
            pool.affine_select(out=blk[:, :, :], in_=blk[:, :, :], compare_op=ALU.is_ge, fill=0.0,
                               base=D1 - 1, pattern=[[0, NC], [D1, H1]], channel_multiplier=-1).then_inc(s_i, 1)

        @block.tensor
        def _(pe):
            pe.wait_ge(s_w, 192)
            for n in range(8):
                c = n % 4
                pe.matmul(ps[n][:, :], w1["wq" if n < 4 else "wk"][:, :], xt[:, c * QC:(c + 1) * QC],
                          start=True, stop=True).then_inc(s_qp, 1)
            pe.wait_ge(s_qa, 4)
            for g in range(4):
                for t in range(4):
                    n = 4 * g + t
                    mm = pe.matmul(ps[g][:, t * P:(t + 1) * P], xt[:, n * P:(n + 1) * P], w1["wv"][:, :],
                                   start=True, stop=True)
                mm.then_inc(s_qp, 1)
            pe.wait_ge(s_gl, 1)
            pe.wait_ge(s_qa, 8)
            pe.matmul(ps[4][:, 0:1], w1["wfg"][:, :], glo[:, :], start=True, stop=True).then_inc(s_gp, 1)
            pe.wait_ge(s_va, 4)
            for c in range(4):
                pe.matmul(ps[c][:, :], w1["wfq"][:, :], mq[:, c * QC:(c + 1) * QC], start=True, stop=True)\
                    .then_inc(s_cp, 1)
            pe.wait_ge(s_bl, 2)
            pe.wait_ge(s_cb, 1)
            for c in range(4):
                pe.wait_ge(s_ca, c + 1)
                if c >= 2:
                    pe.wait_ge(s_pa, 2 * (c - 2) + 2)
                for m, u in enumerate((ublk, zblk)):
                    pe.matmul(ps[4 + 2 * (c % 2) + m][0:CH1, :], u[:, :, :].rearrange("p c h -> p (c h)"),
                              cgate[:, c * QC:(c + 1) * QC], start=True, stop=True).then_inc(s_pp, 1)

        @block.scalar
        def _(act):
            act.wait_ge(s_w, 192)
            for n in range(8):
                c = n % 4
                act.wait_ge(s_qp, n + 1)
                act.activation((mq if n < 4 else mk)[:, c * QC:(c + 1) * QC], ps[n][:, :], ACT.Identity,
                               bias=col["bq" if n < 4 else "bk"][:, 0:1]).then_inc(s_qa, 1)
            act.wait_ge(s_cb, 1)
            for c in range(4):
                act.wait_ge(s_cp, c + 1)
                act.activation(cgate[:, c * QC:(c + 1) * QC], ps[c][:, :], ACT.Tanh, bias=cbias[:, 0:1])\
                    .then_inc(s_ca, 1)
            for c in range(4):
                for m, dst in enumerate((sp_, sz)):
                    act.wait_ge(s_pp, 2 * c + m + 1)
                    act.activation(dst[:, c * QC:(c + 1) * QC], ps[4 + 2 * (c % 2) + m][0:CH1, :], ACT.Sigmoid)\
                        .then_inc(s_pa, 1)

        @block.vector
        def _(dve):
            done = [0]

            def link(ins):
                done[0] += 1
                ins.then_inc(s_dv, 1)
                dve.wait_ge(s_dv, done[0])

            def split(src, dst, n):
                link(dve.tensor_copy(dst[:, 0, :], src))
                link(dve.tensor_tensor(rest[0:n, :], src, dst[:, 0, :], ALU.subtract))
                link(dve.tensor_copy(dst[:, 1, :], rest[0:n, :]))
                ins = dve.tensor_tensor(dst[:, 2, :], rest[0:n, :], dst[:, 1, :], ALU.subtract)
                ins.then_inc(s_pt, 1)
                dve.wait_ge(s_pt, splits.pop(0))

            splits = [1, 2, 3, 4, 5]
            dve.memset(crow[0:1, 3, :], 1.0).then_inc(s_cr, 1)
            dve.memset(crow[0:1, 4, :], -1.0).then_inc(s_cr, 1)
            dve.wait_ge(s_i, 5)
            link(dve.tensor_tensor(dj2[:, :], dj[:, :], dj[:, :], ALU.mult))
            dve.tensor_copy(crow[0:1, 0, :], dj2[:, :]).then_inc(s_cr, 1)
            dve.tensor_copy(crow[0:1, 2, :], dj[:, :]).then_inc(s_cr, 1)
            dve.wait_ge(s_cr, 4)
            dve.tensor_tensor(crow[0:1, 1, :], dj2[:, :], crow[0:1, 0, :], ALU.subtract).then_inc(s_cr, 1)
            dve.wait_ge(s_w, 192)
            for dst, n in ((ublk, "up"), (zblk, "uz")):
                dve.tensor_scalar(dst[:, :, :], blk[:, :, :], col[n][:, 0:1], None, ALU.mult).then_inc(s_bl, 1)
            dve.wait_ge(s_qa, 4)
            link(dve.reduce_sum(glo[:, :], mq[:, :], AX.X))
            dve.tensor_scalar(glo[:, :], glo[:, :], 1.0 / S, None, ALU.mult).then_inc(s_gl, 1)
            for g in range(4):
                dve.wait_ge(s_qp, 9 + g)
                for t in range(4):
                    ins = dve.tensor_tensor(v1[:, 4 * g + t, :], ps[g][:, t * P:(t + 1) * P], bv[:, :], ALU.add)
                ins.then_inc(s_va, 1)
            dve.wait_ge(s_gp, 1)
            link(dve.tensor_tensor(cbias[:, :], ps[4][:, 0:1], col["bfg"][:, :], ALU.add))
            dve.tensor_tensor(cbias[:, :], cbias[:, :], col["bfq"][:, :], ALU.add).then_inc(s_cb, 1)
            link(dve.tensor_scalar(qs[:, :], mq[:, :], 1.0 / math.sqrt(D1), None, ALU.mult))
            split(qs[:, :], parts["q"], P)
            dve.wait_ge(s_qa, 8)
            split(mk[:, :], parts["k"], P)
            dve.wait_ge(s_pa, 8)
            link(dve.reciprocal(f1[:, :], sz[:, :]))
            link(dve.tensor_tensor(na[:, :], f1[:, :], f1[:, :], ALU.mult))
            link(dve.tensor_scalar(na[:, :], na[:, :], -2.0 / (S * S), None, ALU.mult))
            split(na[:, :], gparts["a"], CH1)
            dve.wait_ge(s_ctr, 16)
            link(dve.tensor_scalar(uu[:, :], sp_[:, :], float(S), centre[:, 0:1], ALU.mult, ALU.subtract))
            link(dve.tensor_tensor(f1[:, :], na[:, :], uu[:, :], ALU.mult))
            link(dve.tensor_tensor(uu[:, :], f1[:, :], uu[:, :], ALU.mult))
            link(dve.tensor_scalar(f1[:, :], f1[:, :], -2.0, None, ALU.mult))
            split(f1[:, :], gparts["w1"], CH1)
            split(uu[:, :], gparts["w0"], CH1)

    ctxt = l1.enter_context(nc.sbuf_tensor("ctxt", [P, NT, DM], F32))
    with ExitStack() as ctx:
        def sb(name, shape, dt):
            return ctx.enter_context(nc.sbuf_tensor(name, shape, dt))

        def psum(name, shape, dt=F32):
            return ctx.enter_context(nc.psum_tensor(name, shape, dt))

        def sem(name):
            return ctx.enter_context(nc.semaphore(name))

        RP1 = 8
        CG = 4
        RING = 3
        qrows = sb("qrows", [P, 2, NC, S], BF16)
        v_head = sb("v1_head", [P, 2, NT, 32], F32)
        probs = sb("probs1", [P, RP1, 2, QC], F32)
        maxpart = sb("maxpart1", [P, NT, NC], F32)
        rowmax = sb("rowmax1", [P, 4], F32)
        maxhl = sb("maxhl1", [P, 2, 4], BF16)
        maxrow = sb("maxrow1", [8, 2, P], BF16)
        identb = sb("identb1", [P, P], BF16)
        sel = sb("sel", [P, 16], F32)
        pv_raw = sb("pv_raw1", [P, QC], F32)
        rden = sb("rden1", [P, 4, 1], F32)

        ps_e = psum("ps_e1", [P, 2, 2, QC])
        ps_o = psum("ps_o1", [P, QC])
        ps_r = psum("ps_r1", [P, RING, QC])

        s_q = [[sem(f"s_q{j}{c}") for c in range(NQ)] for j in range(2)]
        s_k = [sem(f"s_k{j}") for j in range(2)]
        s_cst = sem("s_cst1")
        s_cv = sem("s_cv1")
        s_rp = sem("s_rp1")
        s_mt = sem("s_mt1")
        s_rf = sem("s_rf1")
        s_mhl = sem("s_mhl1")
        s_mc = sem("s_mc1")
        s_mrd = [sem(f"s_mrd1{g}") for g in range(2)]
        s_st = sem("s_st1")
        s_ex = sem("s_ex1")
        s_pv = sem("s_pv1")
        s_oc = sem("s_oc1")
        s_vh = sem("s_vh1")
        s_fp = sem("s_fp1")
        s_rd = sem("s_rd1")
        s_fn = sem("s_fn1")
        s_dv = sem("s_dv1")

        MR = 16 * 2 * NC
        KP = NT // 2
        NP1 = NQ * KP
        NCH1 = NT * NC

        NTURN = NP1 // 2
        FN_AT = {5: 0, 9: 1, 13: 2}
        MT_AT = {6: 0, 10: 1, 14: 2}
        LATE_FN, LATE_MT = 1, 2

        def turn_uses(t, first, do_max):
            n = 4 * (t - 1)
            ch = [("max", n + k) for k in range(4)] if do_max and t >= 1 else [None] * 4
            extra = []
            if t in FN_AT:
                extra.append(("fn", FN_AT[t], 0))
            if t == LATE_FN and not first:
                extra.append(("fn", 3, -1))
            if t in MT_AT and do_max:
                extra.append(("mt", MT_AT[t], 1))
            if t == LATE_MT:
                extra.append(("mt", 3, 0))
            return ch, extra

        def ring_uses(first, do_max):
            out = []
            for t in range(NTURN):
                ch, extra = turn_uses(t, first, do_max)
                out += [c for c in ch[0:3] if c] + extra + [c for c in ch[3:] if c]
            if do_max:
                out += [("max", n) for n in range(4 * (NTURN - 1), NCH1)]
            return out

        BEFORE = [u for g in range(4) for u in [("max", n) for n in range(16 * g, 16 * g + 16)] + [("mt", g, 1)]][:-1]
        FULL = len(ring_uses(False, True))
        SHIFT = len(BEFORE) + len(ring_uses(True, True)) - FULL
        assert FULL % RING == 0

        def ring_base(h, first):
            return (len(BEFORE), len(BEFORE) % RING) if first else (SHIFT + FULL * h, SHIFT % RING)

        def load_q(eng, h, j, c):
            cols = slice(c * QC, (c + 1) * QC)
            eng.dma_start(qrows[0:R_A, j, :, cols],
                          qd[bass.ds(h, 1), :, cols].rearrange("a (r c) s -> (a r) c s", c=1)
                          .to_broadcast([R_A, NC, QC])).then_inc(s_q[j][c], 16)
            eng.dma_start(qrows[R_A:R_M, j, :, cols],
                          gd[bass.ds(h, 1), :, :, cols].rearrange("a r c s -> (a r) c s")).then_inc(s_q[j][c], 16)

        def load_k(eng, h, j):
            eng.dma_start(krows[0:R_A, j, :], kd[bass.ds(h, 1)].rearrange("a r s -> (a r) s")).then_inc(s_k[j], 16)

        block = ctx.enter_context(nc.Block())

        @block.sync
        def _(sp):
            load_k(sp, 0, 0)
            for h in range(2):
                if h:
                    load_k(sp, h, h)
                for c in range(NQ):
                    load_q(sp, h, h, c)

            def place_max(h, j, g):
                sp.wait_ge(s_mc, 4 * h + g + 1)
                for r in range(2):
                    for c in range(NC):
                        sp.dma_start(qrows[R_M + r:R_M + r + 1, j, c, g * QC:(g + 1) * QC],
                                     maxrow[4 * r:4 * r + 4, g % 2, :]).then_inc(s_mrd[g % 2], 16)

            with sp.Fori(0, H1 - 1, 2) as i:
                for j in range(2):
                    for g in range(4):
                        place_max(i + j, j, g)

        @block.gpsimd
        def _(pool):
            pool.memset(sel[:, :], 0.0).then_inc(s_cst, 1)
            pool.wait_ge(s_cst, 1)
            for g in range(CG):
                pool.affine_select(out=sel[:, :], in_=sel[:, :], compare_op=ALU.not_equal, fill=1.0,
                                   base=-32 * g, pattern=[[-1, 16]], channel_multiplier=1).then_inc(s_cst, 1)
                pool.wait_ge(s_cst, 2 + g)

        @block.scalar
        def _(act):
            act.sem_inc(s_ex, 2)
            act.sem_inc(s_oc, 1)

            def exps(h, p):
                act.wait_ge(s_st, NP1 * h + p + 1)
                act.wait_ge(s_pv, NP1 * h + p + 1)
                act.activation(probs[:, p % RP1], ps_e[:, p % 2], ACT.Exp).then_inc(s_ex, 1)

            def copy_pv(h, qc):
                act.wait_ge(s_pv, NP1 * h + KP * (qc + 1) + RP1)
                act.wait_ge(s_fp, 4 * h + qc + 1)
                act.activation(pv_raw[:, :], ps_o[:, :], ACT.Copy).then_inc(s_oc, 1)

            def step(h, j, first, more):
                for p in range(NP1):
                    exps(h, p)
                    if p in (8, 16, 24) and more:
                        load_q(act, h + 2, j, p // 8 - 1)
                    if p in (9, 17, 25):
                        copy_pv(h, p // 8 - 1)
                    if p == 1 and not first:
                        copy_pv(h - 1, 3)
                if more:
                    load_k(act, h + 2, j)
                    load_q(act, h + 2, j, 3)

            step(0, 0, True, True)
            with act.Fori(1, H1 - 4, 2) as i:
                step(i, 1, False, True)
                step(i + 1, 0, False, True)
            step(H1 - 3, 1, False, True)
            step(H1 - 2, 0, False, False)
            step(H1 - 1, 1, False, False)
            copy_pv(H1 - 1, 3)

        @block.tensor
        def _(pe):
            pe.sem_inc(s_pv, RP1)
            pe.sem_inc(s_fp, 1)

            def max_chunk(h, j, n, use, bank):
                qt, c = divmod(n, NC)
                if n == 0:
                    pe.wait_ge(s_k[j], 8 * (h - j) + 16)
                if n % (4 * NC) == 0:
                    pe.wait_ge(s_q[j][qt // 4], 16 * (h - j) + 32)
                pe.wait_ge(s_rf, use + 1)
                pe.matmul(ps_r[:, bank, :], qrows[0:R_M, j, c, qt * P:(qt + 1) * P],
                          krows[0:R_M, j, c * KB:(c + 1) * KB], start=True, stop=True).then_inc(s_rp, 1)

            def max_transpose(h, g, use, bank):
                pe.wait_ge(s_mhl, 4 * h + g + 1)
                pe.wait_ge(s_rf, use + 1)
                pe.transpose(ps_r[:, bank, :].bitcast(BF16)[0:8, 0:P], maxhl[:, :, :].rearrange("p r t -> p (r t)"),
                             identb[:, :]).then_inc(s_mt, 1)

            def scores(h, j, p):
                qc, kp = divmod(p, KP)
                if kp == 0:
                    pe.wait_ge(s_mrd[qc % 2], MR * (2 * h + qc // 2 + 1))
                pe.wait_ge(s_ex, NP1 * h + p + 1)
                for u in range(2):
                    kt = 2 * kp + u
                    mm = pe.matmul(ps_e[:, p % 2, u], krows[0:R_END, j, kt * P:(kt + 1) * P],
                                   qrows[0:R_END, j, kt * P // KB, qc * QC:(qc + 1) * QC], start=True, stop=True)
                mm.then_inc(s_st, 1)

            def pv(h, j, p):
                qc, kp = divmod(p, KP)
                pe.wait_ge(s_ex, NP1 * h + p + 4)
                if p == 0:
                    pe.wait_ge(s_vh, h + 1)
                if kp == 0:
                    pe.wait_ge(s_oc, 4 * h + qc + 1)
                for u in range(CG):
                    kt = 2 * kp + u
                    mm = pe.matmul(ps_o[32 * u:32 * u + 32, :], v_head[:, j, kt, :],
                                   probs[:, (p + u // 2) % RP1, u % 2], start=kp == 0, stop=kp == KP - 2,
                                   skip_group_check=True)
                mm.then_inc(s_pv, 2)

            def finish(h, qc, use, bank):
                pe.wait_ge(s_oc, 4 * h + qc + 2)
                pe.wait_ge(s_rf, use + 1)
                for t in range(4):
                    mm = pe.matmul(ps_r[:, bank, 16 * t:16 * t + 16], pv_raw[:, t * P:(t + 1) * P], sel[:, :],
                                   start=True, stop=True)
                mm.then_inc(s_fp, 1)

            pe.wait_ge(s_cst, 5)
            pe.wait_ge(s_cv, 2)
            for at, use in enumerate(BEFORE):
                if use[0] == "max":
                    max_chunk(0, 0, use[1], at, at % RING)
                else:
                    max_transpose(0, use[1], at, at % RING)

            def step(h, j, first, do_max):
                base, mod = ring_base(h, first)
                local = [0]

                def ring(use):
                    at, bank = base + local[0], (mod + local[0]) % RING
                    local[0] += 1
                    if use[0] == "max":
                        max_chunk(h + 1, 1 - j, use[1], at, bank)
                    elif use[0] == "mt":
                        max_transpose(h + use[2], use[1], at, bank)
                    else:
                        finish(h + use[2], use[1], at, bank)

                for t in range(NTURN):
                    ch, extra = turn_uses(t, first, do_max)
                    if ch[0]:
                        ring(ch[0])
                    scores(h, j, 2 * t)
                    if ch[1]:
                        ring(ch[1])
                    scores(h, j, 2 * t + 1)
                    if ch[2]:
                        ring(ch[2])
                    for use in extra:
                        ring(use)
                    if t >= 1:
                        pv(h, j, 2 * t - 2)
                    elif not first:
                        pv(h - 1, 1 - j, NP1 - 2)
                    if ch[3]:
                        ring(ch[3])
                if do_max:
                    for n in range(4 * (NTURN - 1), NCH1):
                        ring(("max", n))
                assert local[0] == len(ring_uses(first, do_max))

            step(0, 0, True, True)
            with pe.Fori(1, H1 - 4, 2) as i:
                step(i, 1, False, True)
                step(i + 1, 0, False, True)
            step(H1 - 3, 1, False, True)
            step(H1 - 2, 0, False, True)
            step(H1 - 1, 1, False, False)
            pv(H1 - 1, 1, NP1 - 2)
            finish(H1 - 1, 3, SHIFT + FULL * (H1 - 1) + len(ring_uses(False, False)),
                   (SHIFT + len(ring_uses(False, False))) % RING)

        @block.vector
        def _(dve):
            dve.tensor_copy(identb[:, :], ident[:, :]).then_inc(s_cv, 1)
            dve.memset(v_head[:, :, :, :], 0.0).then_inc(s_dv, 1)
            dve.wait_ge(s_dv, 1)
            dve.memset(v_head[:, :, :, D1:D1 + 1], 1.0).then_inc(s_cv, 1)
            dve.sem_inc(s_rf, RING)

            def take_max(h, n, bank):
                qt, c = divmod(n, NC)
                dve.wait_ge(s_rp, NCH1 * h + n + 1)
                dve.reduce_max(maxpart[:, qt, c:c + 1], ps_r[:, bank, :], AX.X).then_inc(s_rf, 1)

            def split_max(h, g, read):
                dve.wait_ge(s_rf, read)
                dve.reduce_max(rowmax[:, :], maxpart[:, 4 * g:4 * g + 4, :], AX.X).then_inc(s_dv, 1)
                dve.wait_ge(s_dv, 12 * h + 3 * g + 2)
                dve.tensor_scalar(rowmax[:, :], rowmax[:, :], HEADROOM, None, ALU.add).then_inc(s_dv, 1)
                dve.wait_ge(s_dv, 12 * h + 3 * g + 3)
                dve.tensor_copy(maxhl[:, 0, :], rowmax[:, :]).then_inc(s_dv, 1)
                dve.wait_ge(s_dv, 12 * h + 3 * g + 4)
                dve.tensor_tensor(maxhl[:, 1, :], rowmax[:, :], maxhl[:, 0, :], ALU.subtract).then_inc(s_mhl, 1)

            def max_out(h, g, bank):
                dve.wait_ge(s_mt, 4 * h + g + 1)
                if not isinstance(h, int) or 4 * h + g >= 2:
                    dve.wait_ge(s_mrd[g % 2], MR * (2 * h + g // 2))
                dve.tensor_copy(maxrow[:, g % 2, :], ps_r[:, bank, :].bitcast(BF16)[0:8, 0:P]).then_inc(s_mc, 1)
                dve.wait_ge(s_mc, 4 * h + g + 1)
                dve.sem_inc(s_rf, 1)

            def normalise(h, qc, bank):
                dve.wait_ge(s_fp, 4 * h + qc + 2)
                x = ps_r[:, bank, 0:64].rearrange("p (t c) -> p t c", c=16)
                dve.reciprocal(rden[:, :, :], x[:, :, D1:D1 + 1]).then_inc(s_rd, 1)
                dve.wait_ge(s_rd, 4 * h + qc + 1)
                dve.tensor_tensor(ctxt[:, 4 * qc:4 * qc + 4, bass.ds(D1 * h, D1)], x[:, :, 0:D1],
                                  rden[:, :, :].to_broadcast([P, 4, D1]), ALU.mult).then_inc(s_fn, 1)
                dve.wait_ge(s_fn, 4 * h + qc + 1)
                dve.sem_inc(s_rf, 1)

            def read_ring(h, j, uses, base, mod):
                for k, use in enumerate(uses):
                    bank = (mod + k) % RING
                    if use[0] == "max":
                        take_max(h, use[1], bank)
                        if use[1] % 16 == 15:
                            split_max(h, use[1] // 16, base + k + 1 + RING)
                    elif use[0] == "mt":
                        max_out(h - 1 + use[2], use[1], bank)
                    else:
                        normalise(h - 1 + use[2], use[1], bank)
                    if use == ("max", 20):
                        if not isinstance(h, int) or h >= 2:
                            dve.wait_ge(s_pv, NP1 * (h - 1) + RP1)
                        dve.tensor_copy(v_head[:, j, :, 0:D1], v1[:, :, bass.ds(h * D1, D1)]).then_inc(s_vh, 1)

            def step(h, j, first, do_max):
                base, mod = ring_base(h, first)
                read_ring(h + 1, 1 - j, ring_uses(first, do_max), base, mod)

            read_ring(0, 0, BEFORE, 0, 0)
            step(0, 0, True, True)
            with dve.Fori(1, H1 - 4, 2) as i:
                step(i, 1, False, True)
                step(i + 1, 0, False, True)
            step(H1 - 3, 1, False, True)
            step(H1 - 2, 0, False, True)
            step(H1 - 1, 1, False, False)
            normalise(H1 - 1, 3, (SHIFT + len(ring_uses(False, False))) % RING)

    with ExitStack() as ctx:
        def sem(name):
            return ctx.enter_context(nc.semaphore(name))

        wo = ctx.enter_context(nc.sbuf_tensor("l1_wo", [P, DM], F32))
        bo = ctx.enter_context(nc.sbuf_tensor("l1_bo", [P, 1], F32))
        xb = ctx.enter_context(nc.sbuf_tensor("x_bias", [P, S], F32))
        ct = ctx.enter_context(nc.sbuf_tensor("ct", [P, S], F32))
        ps = [ctx.enter_context(nc.psum_tensor(f"ps_wo{n}", [P, QC], F32)) for n in range(8)]
        s_w = sem("s_wo1")
        s_tp = sem("s_tp1")
        s_tc = sem("s_tc1")
        s_op = sem("s_op1")
        s_xb = sem("s_xb1")
        s_oy = sem("s_oy1")
        block = ctx.enter_context(nc.Block())

        @block.sync
        def _(sp):
            sp.dma_start(wo[:, :], a["L1_attn_wo"]).then_inc(s_w, 16)
            with nc.allow_non_contiguous_dma(reason="small column"):
                sp.dma_start(bo[:, :], a["L1_attn_bo"].rearrange("(m a) -> m a", a=1)).then_inc(s_w, 16)

        @block.tensor
        def _(pe):
            for g in range(4):
                for t in range(4):
                    tr = pe.transpose(ps[g][:, t * P:(t + 1) * P], ctxt[:, 4 * g + t, :], ident[:, :])
                tr.then_inc(s_tp, 1)
            pe.wait_ge(s_w, 32)
            for g in range(4):
                pe.wait_ge(s_tc, g + 1)
                pe.matmul(ps[4 + g][:, :], wo[:, :], ct[:, g * QC:(g + 1) * QC], start=True, stop=True)\
                    .then_inc(s_op, 1)

        @block.scalar
        def _(act):
            for g in range(4):
                act.wait_ge(s_tp, g + 1)
                act.activation(ct[:, g * QC:(g + 1) * QC], ps[g][:, :], ACT.Copy).then_inc(s_tc, 1)

        @block.vector
        def _(dve):
            dve.wait_ge(s_w, 32)
            dve.tensor_scalar(xb[:, :], xt[:, :], bo[:, 0:1], None, ALU.add).then_inc(s_xb, 1)
            dve.wait_ge(s_xb, 1)
            for g in range(4):
                cols = slice(g * QC, (g + 1) * QC)
                dve.wait_ge(s_op, g + 1)
                dve.tensor_tensor(yt[:, cols], ps[4 + g][:, :], xb[:, cols], ALU.add).then_inc(s_oy, 1)
            dve.wait_ge(s_oy, 4)

    l1.close()
    norm_block(nc, "n2", yt, x_sb, xt, ident)

    with ExitStack() as ctx:
        def sb(name, shape):
            return ctx.enter_context(nc.sbuf_tensor(name, shape, F32))

        def sem(name):
            return ctx.enter_context(nc.semaphore(name))

        RANK, DD = a["L1_ffn_lora_down"].shape
        UD = a["L1_ffn_lora_up"].shape[0]
        w_raw = sb("w_raw", [P, DM])
        w_t = sb("w_t", [P, DM])
        ua_raw = sb("ua_raw", [P, UD])
        ua_t = sb("ua_t", [UD, P])
        lu_raw = sb("lu_raw", [UD, RANK])
        lu_t = sb("lu_t", [RANK, UD])
        ld_raw = sb("ld_raw", [RANK, DD])
        ld_t = sb("ld_t", [DD, RANK])
        da = sb("da", [DD, DM])
        inner = sb("inner", [RANK, DM])
        outer = sb("outer", [UD, DM])
        bcol = sb("bcol", [P, 1])
        xb = sb("x_bias2", [P, S])
        ps = [ctx.enter_context(nc.psum_tensor(f"ps_l{n}", [P, QC], F32)) for n in range(8)]
        s_w = sem("s_w2")
        s_tp = sem("s_tp2")
        s_tc = sem("s_tc2")
        s_lp = sem("s_lp2")
        s_lc = sem("s_lc2")
        s_op = sem("s_op2")
        s_xb = sem("s_xb2")
        s_oy = sem("s_oy2")
        block = ctx.enter_context(nc.Block())
        TURN = ((w_raw, w_t, P, DM), (ua_raw, ua_t, P, UD), (lu_raw, lu_t, UD, RANK), (ld_raw, ld_t, RANK, DD))

        @block.sync
        def _(sp):
            for n, dst in (("W", w_raw), ("up_aux", ua_raw), ("lora_up", lu_raw), ("lora_down", ld_raw),
                           ("down_aux", da)):
                sp.dma_start(dst[:, :], a[f"L1_ffn_{n}"]).then_inc(s_w, 16)
            with nc.allow_non_contiguous_dma(reason="small column"):
                sp.dma_start(bcol[:, :], a["L1_ffn_b"].rearrange("(m a) -> m a", a=1)).then_inc(s_w, 16)

        @block.tensor
        def _(pe):
            pe.wait_ge(s_w, 96)
            for n, (raw, _, rows, cols) in enumerate(TURN):
                pe.transpose(ps[n][0:cols, 0:rows], raw[:, :], ident[0:rows, 0:rows]).then_inc(s_tp, 1)
            pe.wait_ge(s_tc, 4)
            pe.matmul(ps[4][0:RANK, 0:DM], ld_t[:, :], da[:, :], start=True, stop=True).then_inc(s_lp, 1)
            pe.wait_ge(s_lc, 1)
            pe.matmul(ps[5][0:UD, 0:DM], lu_t[:, :], inner[:, :], start=True, stop=True).then_inc(s_lp, 1)
            pe.wait_ge(s_lc, 2)
            pe.matmul(ps[6][:, 0:P], outer[:, :], ua_t[:, :], start=True, stop=True).then_inc(s_lp, 1)
            pe.wait_ge(s_lc, 3)
            for g in range(4):
                pe.matmul(ps[g][:, :], w_t[:, :], xt[:, g * QC:(g + 1) * QC], start=True, stop=True)\
                    .then_inc(s_op, 1)

        @block.vector
        def _(dve):
            dve.wait_ge(s_w, 96)
            dve.tensor_scalar(xb[:, :], xt[:, :], bcol[:, 0:1], None, ALU.add).then_inc(s_xb, 1)
            for n, (_, dst, rows, cols) in enumerate(TURN):
                dve.wait_ge(s_tp, n + 1)
                dve.tensor_copy(dst[:, :], ps[n][0:cols, 0:rows]).then_inc(s_tc, 1)
            for n, (dst, rows) in enumerate(((inner, RANK), (outer, UD))):
                dve.wait_ge(s_lp, n + 1)
                dve.tensor_copy(dst[:, :], ps[4 + n][0:rows, 0:DM]).then_inc(s_lc, 1)
            dve.wait_ge(s_lp, 3)
            dve.wait_ge(s_tc, 4)
            dve.tensor_tensor(w_t[:, :], w_t[:, :], ps[6][:, 0:P], ALU.add).then_inc(s_lc, 1)
            dve.wait_ge(s_xb, 1)
            for g in range(4):
                cols = slice(g * QC, (g + 1) * QC)
                dve.wait_ge(s_op, g + 1)
                dve.tensor_tensor(yt[:, cols], ps[g][:, :], xb[:, cols], ALU.add).then_inc(s_oy, 1)
            dve.wait_ge(s_oy, 4)

    norm_block(nc, "n3", yt, x_sb, xt, ident, out_dram)
    persist.close()


def kernel(**inputs):
    import concourse.bacc as _bacc
    from concourse.bass_utils import run_bass_kernel_spmd as _run

    nc = _bacc.Bacc("TRN2", target_bir_lowering=False, num_devices=1)
    arrays, args = {}, {}
    for name in sorted(inputs):
        v = np.ascontiguousarray(inputs[name])
        arrays[f"in_{name}"] = v
        args[name] = nc.dram_tensor(f"in_{name}", v.shape, mybir.dt.from_np(v.dtype), kind="ExternalInput").ap()
    out = nc.dram_tensor("out_0", (1, S, DM), F32, kind="ExternalOutput").ap()
    build(nc, args, out)
    r = _run(nc, [arrays], core_ids=[0])
    return r.results[0]["out_0"]
```

```python
import math
from contextlib import ExitStack

import numpy as np
import concourse.bass as bass
from concourse import mybir

F32 = mybir.dt.float32
F16 = mybir.dt.float16
BF16 = mybir.dt.bfloat16
ALU = mybir.AluOpType
ACT = mybir.ActivationFunctionType
AX = mybir.AxisListType

P = 128
S = 2048
DM = 128
NT = S // P
QC = 512
NQ = S // QC
H0, D0 = 16, 64
H1, D1 = 16, 8
HID = 512
RP = 4
NEG = -1e30
EPS = 1e-5
HEADROOM = 20.0
assert DM == P and 2 * D0 == P and H1 * D1 == DM


def norm_block(nc, tag, yt, x_sb, xt, ident, out_dram=None, tokens_first=False):
    with ExitStack() as ctx:
        def sb(name, shape, dt):
            return ctx.enter_context(nc.sbuf_tensor(f"{name}_{tag}", shape, dt))

        def sem(name):
            return ctx.enter_context(nc.semaphore(f"{name}_{tag}"))

        stats = sb("stats", [P, NT, 6], F32)
        mv = sb("mv", [P, NT, 2], F32)
        veps = sb("veps", [P, NT], F32)
        root = sb("root", [P, NT], F32)
        rstd = sb("rstd", [P, NT], F32)
        t1 = sb("t1", [P, NT], F32)
        ps_y = ctx.enter_context(nc.psum_tensor(f"ps_y_{tag}", [P, 4, 4, P], F32))
        ps_t = ctx.enter_context(nc.psum_tensor(f"ps_t_{tag}", [P, 4, QC], F32))
        s_y = sem("s_y")
        s_ve = sem("s_ve")
        s_rt = sem("s_rt")
        s_n = sem("s_n")
        s_xp = sem("s_xp")
        s_xc = sem("s_xc")
        s_dv = sem("s_dv")
        s_out = sem("s_out")
        block = ctx.enter_context(nc.Block())

        def y_tile(n):
            return yt[:, n * P:(n + 1) * P] if tokens_first else ps_y[:, n // 4, n % 4, :]

        @block.tensor
        def _(pe):
            for g in range(0 if tokens_first else 4):
                for t in range(4):
                    tr = pe.transpose(ps_y[:, g, t, :], yt[:, (4 * g + t) * P:(4 * g + t + 1) * P], ident[:, :])
                tr.then_inc(s_y, 1)
            if out_dram is None:
                for g in range(4):
                    pe.wait_ge(s_n, 4 * g + 4)
                    for t in range(4):
                        tr = pe.transpose(ps_t[:, g, t * P:(t + 1) * P], x_sb[:, 4 * g + t, :], ident[:, :])
                    tr.then_inc(s_xp, 1)

        @block.scalar
        def _(act):
            for g in range(4):
                act.wait_ge(s_ve, g + 1)
                act.activation(root[:, 4 * g:4 * g + 4], veps[:, 4 * g:4 * g + 4], ACT.Sqrt).then_inc(s_rt, 1)
            if out_dram is None:
                for g in range(4):
                    act.wait_ge(s_xp, g + 1)
                    act.activation(xt[:, g * QC:(g + 1) * QC], ps_t[:, g, :], ACT.Copy).then_inc(s_xc, 1)
                act.wait_ge(s_xc, 4)

        @block.vector
        def _(dve):
            done = [0]

            def link(ins):
                done[0] += 1
                ins.then_inc(s_dv, 1)
                dve.wait_ge(s_dv, done[0])

            def statistics(g):
                if not tokens_first:
                    dve.wait_ge(s_y, g + 1)
                for t in range(4):
                    ins = dve.bn_stats(stats[:, 4 * g + t, :], y_tile(4 * g + t))
                link(ins)
                for t in range(4):
                    ins = dve.bn_aggr(mv[:, 4 * g + t, :], stats[:, 4 * g + t, :])
                link(ins)
                dve.tensor_scalar(veps[:, 4 * g:4 * g + 4], mv[:, 4 * g:4 * g + 4, 1], EPS, None, ALU.add)\
                    .then_inc(s_ve, 1)

            def apply(g):
                c = slice(4 * g, 4 * g + 4)
                dve.wait_ge(s_rt, g + 1)
                dve.wait_ge(s_ve, g + 1)
                link(dve.reciprocal(rstd[:, c], root[:, c]))
                link(dve.tensor_tensor(t1[:, c], rstd[:, c], rstd[:, c], ALU.mult))
                link(dve.tensor_tensor(t1[:, c], t1[:, c], veps[:, c], ALU.mult))
                link(dve.tensor_scalar(t1[:, c], t1[:, c], -0.5, 1.5, ALU.mult, ALU.add))
                link(dve.tensor_tensor(rstd[:, c], rstd[:, c], t1[:, c], ALU.mult))
                for t in range(4):
                    n = 4 * g + t
                    dve.tensor_scalar(x_sb[:, n, :], y_tile(n), mv[:, n, 0:1], rstd[:, n:n + 1],
                                      ALU.subtract, ALU.mult).then_inc(s_n, 1)

            statistics(0)
            for g in range(4):
                if g < 3:
                    statistics(g + 1)
                apply(g)

        if out_dram is not None:
            @block.sync
            def _(sp):
                for g in range(4):
                    sp.wait_ge(s_n, 4 * g + 4)
                    sp.dma_start(out_dram.rearrange("(t p) d -> p t d", p=P)[:, 4 * g:4 * g + 4, :],
                                 x_sb[:, 4 * g:4 * g + 4, :]).then_inc(s_out, 16)
                sp.wait_ge(s_out, 64)



def build(nc, a, out):
    x_dram = a["L0_attn_x"].rearrange("b s d -> (b s) d")
    out_dram = out.rearrange("b s d -> (b s) d")
    persist = ExitStack()
    x_sb = persist.enter_context(nc.sbuf_tensor("x_sb", [P, NT, DM], F32))
    xt = persist.enter_context(nc.sbuf_tensor("xt", [P, S], F32))
    yt = persist.enter_context(nc.sbuf_tensor("yt", [P, S], F32))
    ident = persist.enter_context(nc.sbuf_tensor("ident", [P, P], F32))
    with ExitStack() as ctx:
        def sb(name, shape, dt):
            return ctx.enter_context(nc.sbuf_tensor(name, shape, dt))

        def psum(name, shape, dt=F32):
            return ctx.enter_context(nc.psum_tensor(name, shape, dt))

        def sem(name):
            return ctx.enter_context(nc.semaphore(name))

        v_all = sb("v_all", [P, NT, H0 * D0], F32)
        v_head = sb("v_head", [P, 2, NT, D0], F32)
        wv = sb("wv", [P, H0, D0], F32)
        vbias = sb("vbias", [P, H0 * D0], F32)
        wqk = sb("wqk", [P, 2, 2 * D0], F32)
        wo2 = sb("wo2", [P, 2, P], F32)
        obias = sb("obias", [P, 1, P], F32)
        qkbias = sb("qkbias", [P, H0], F32)
        qkbias_head = sb("qkbias_head", [P, 2], F32)
        qkscale = sb("qkscale", [P, 1], F32)
        qk32 = sb("qk32", [P, 2, QC], F32)
        qk_hi = sb("qk_hi", [P, S], F16)
        qk_lo = sb("qk_lo", [P, S], F16)
        qq = sb("qq", [P, 2, S], F16)
        kk = sb("kk", [P, 2, S], F16)
        qm = sb("qm", [P, 2, S], F16)
        km = sb("km", [P, 2, S], F16)
        maxpart = sb("maxpart", [P, NT, NQ], F32)
        rowmax = sb("rowmax", [P, 4], F32)
        maxhl = sb("maxhl", [P, 2, 4], F16)
        maxrow = sb("maxrow", [8, 2, P], F16)
        probs = sb("probs", [P, RP, 2, QC], F32)
        acc = sb("acc", [P, 2, 2, QC], F32)
        accsum = sb("accsum", [P, QC], F32)
        rden = sb("rden", [P, 4], F32)
        pv_raw = sb("pv_raw", [P, 2, QC], F32)
        ones = sb("ones", [P, 1], F32)
        zeros = sb("zeros", [P, 1, 1], F32)
        mask = sb("mask", [P, P], BF16)
        allneg = sb("allneg", [P, P], BF16)
        identb = sb("identb", [P, P], BF16)
        identh = sb("identh", [P, P], F16)

        ps_e = psum("ps_e", [P, 2, 2, QC])
        ps_m = psum("ps_m", [P, 2, QC])
        ps_o = psum("ps_o", [P, QC])
        ps_x = psum("ps_x", [P, QC])
        ps_xh = ps_x[:, :].bitcast(F16)
        y_tok = yt[:, :].rearrange("p (t d) -> p t d", d=P)

        s_ld = sem("s_ld")
        s_ldx = sem("s_ldx")
        s_cst = sem("s_cst")
        s_cstv = sem("s_cstv")
        s_xt = sem("s_xt")
        s_xtc = sem("s_xtc")
        s_vp = sem("s_vp")
        s_vc = sem("s_vc")
        s_wqk = [sem(f"s_wqk{n}") for n in range(2)]
        s_wo = [sem(f"s_wo{n}") for n in range(2)]
        s_qkp = sem("s_qkp")
        s_t32 = sem("s_t32")
        s_lo = sem("s_lo")
        s_qkd = [sem(f"s_qkd{n}") for n in range(2)]
        s_mxp = sem("s_mxp")
        s_mxr = sem("s_mxr")
        s_mhl = sem("s_mhl")
        s_mc = sem("s_mc")
        s_mrd = [sem(f"s_mrd{n}") for n in range(2)]
        s_st = sem("s_st")
        s_ex = sem("s_ex")
        s_pv = sem("s_pv")
        s_ad = sem("s_ad")
        s_oc = sem("s_oc")
        s_vh = sem("s_vh")
        s_xf = sem("s_xf")
        s_sb = sem("s_sb")
        s_hv = sem("s_hv")
        s_rd = sem("s_rd")
        s_op = sem("s_op")
        s_ac = sem("s_ac")
        s_dv = sem("s_dv")
        s_qb = sem("s_qb")
        s_mt = sem("s_mt")

        PAIRS = [(qc, kp) for qc in range(NQ) for kp in range(2 * qc + 2)]
        NP = len(PAIRS)
        LAST = [n for n, (qc, kp) in enumerate(PAIRS) if kp == 2 * qc + 1]
        CH = [(qt, c) for qt in range(NT) for c in range(qt // 4 + 1)]
        NCH = len(CH)
        GEND = [sum(4 * (g + 1) for g in range(k + 1)) for k in range(4)]
        CH_END = [0, 0, 2, 4, 6, 8, 10, 12, 14, 16, 18, 20, 22, 24, 27, 30, 33, 36, 38, NCH]
        SLOT_CH = {p: (CH_END[p - 1], CH_END[p]) for p in range(2, NP)}
        USES = {1: ("mt", 3), 2: ("sb", 3), 4: ("op", 3), 5: ("sb", 0), 6: ("mt", 0), 7: ("op", 0), 8: ("mt", 1),
                9: ("sb", 1), 10: ("qk", 0), 11: ("op", 1), 12: ("qk", 1), 13: ("qk", 2), 14: ("mt", 2),
                15: ("sb", 2), 16: ("qk", 3), 17: ("op", 2)}

        def use_at(p, fin, do_max, do_proj):
            if p not in USES:
                return None
            kind, g = USES[p]
            if g == 3 and kind != "qk":
                return (kind, g, 0 if kind == "mt" else -1) if fin else None
            if kind == "mt":
                return (kind, g, 1) if do_max else None
            if kind == "qk":
                return (kind, g, 2) if do_proj else None
            return kind, g, 0

        def count_uses(flags):
            return sum(use_at(p, *flags) is not None for p in range(NP))

        FIRST, FULL, NEXT_LAST, LAST_HEAD = (False, True, True), (True, True, True), (True, True, False), \
            (True, False, False)
        PRE_USES = 8 + 4

        def uses_before(h, flags, p):
            inside = sum(use_at(q, *flags) is not None for q in range(p))
            if isinstance(h, int) and h == 0:
                return PRE_USES + inside
            late = count_uses(NEXT_LAST) - count_uses(FULL) if isinstance(h, int) and h == H0 - 1 else 0
            return PRE_USES + count_uses(FIRST) + (h - 1) * count_uses(FULL) + late + inside

        END_USES = PRE_USES + count_uses(FIRST) + (H0 - 3) * count_uses(FULL) + count_uses(NEXT_LAST) \
            + count_uses(LAST_HEAD)

        def diag(qc, kt):
            return kt - 4 * qc if kt >= 4 * qc else None

        def off(qc, kt):
            j = diag(qc, kt)
            return 0 if j is None or kt < 2 else P * j

        def load_wqk(eng, h, j):
            for r, name in enumerate(("L0_attn_Q_w", "L0_attn_K_w")):
                eng.dma_start(wqk[:, j, D0 * r:D0 * r + D0], a[name][bass.ds(h, 1)].rearrange("a m d -> m (a d)"))\
                    .then_inc(s_wqk[j], 16)

        def load_wo(eng, h, j):
            for r in range(2):
                eng.dma_start(wo2[D0 * r:D0 * r + D0, j, :],
                              a["L0_attn_O_w"][bass.ds(h, 1)].rearrange("a d m -> d (a m)")).then_inc(s_wo[j], 16)

        block = ctx.enter_context(nc.Block())

        @block.sync
        def _(sp):
            sp.dma_start(x_sb[:, :, :], x_dram.rearrange("(t p) d -> p t d", p=P)).then_inc(s_ldx, 16)
            sp.dma_start(wv[:, :, :], a["L0_attn_V_w"].rearrange("h m d -> m h d")).then_inc(s_ld, 16)

            for h in range(2):
                load_wqk(sp, h, h)
            load_wo(sp, 0, 0)
            vb = a["L0_attn_V_b"].rearrange("h d -> (h d)").rearrange("(a n) -> a n", a=1)
            sp.dma_start(vbias[:, :], vb.to_broadcast([P, H0 * D0])).then_inc(s_ld, 16)
            with nc.allow_non_contiguous_dma(reason="small bias columns"):
                sp.dma_start(qkbias[0:D0, :], a["L0_attn_Q_b"].rearrange("h d -> d h")).then_inc(s_ld, 16)
                sp.dma_start(qkbias[D0:P, :], a["L0_attn_K_b"].rearrange("h d -> d h")).then_inc(s_ld, 16)
            sp.dma_start(obias[:, 0, :], a["L0_attn_O_b"].rearrange("(a m) -> a m", a=1).to_broadcast([P, P]))\
                .then_inc(s_ld, 16)

            def place_operands(h, j, read=None):
                made = 4 * h + 4
                if read is not None and not isinstance(read, int):
                    made, read = sp.snap(made), sp.snap(read)
                sp.wait_ge(s_lo, made)
                if read is not None:
                    sp.wait_ge(s_st, read)
                for dst, src in ((qq[0:D0, j], qk_hi[0:D0]), (qq[D0:P, j], qk_lo[0:D0]), (kk[0:D0, j], qk_hi[D0:P]),
                                 (kk[D0:P, j], qk_hi[D0:P]), (qm[0:D0, j], qk_hi[0:D0]), (km[0:D0, j], qk_lo[D0:P])):
                    sp.dma_start(dst, src).then_inc(s_qkd[j], 16)

            def place_max(h, j, g):
                sp.wait_ge(s_mc, 4 * h + g + 1)
                for r in range(2):
                    sp.dma_start(qm[D0 + r:D0 + r + 1, j, g * QC:(g + 1) * QC].rearrange("a (t q) -> a t q", q=P),
                                 maxrow[4 * r:4 * r + 4, g % 2, :])\
                        .then_inc(s_mrd[g % 2], 16)

            place_operands(0, 0)
            place_operands(1, 1)
            for g in range(4):
                place_max(0, 0, g)

            def step(h, j, flags):
                fin, do_max, do_proj = flags
                if fin:
                    place_max(h, j, 3)
                if do_max:
                    for g in range(3):
                        place_max(h + 1, 1 - j, g)
                if do_proj:
                    place_operands(h + 2, j, NP * h + NP)

            step(0, 0, FIRST)
            with sp.Fori(1, H0 - 4, 2) as i:
                step(i, 1, FULL)
                step(i + 1, 0, FULL)
            step(H0 - 3, 1, FULL)
            step(H0 - 2, 0, NEXT_LAST)
            step(H0 - 1, 1, LAST_HEAD)

        @block.gpsimd
        def _(pool):
            pool.memset(ident[:, :], 0.0).then_inc(s_cst, 1)
            pool.memset(mask[:, :], 0.0).then_inc(s_cst, 1)
            pool.memset(allneg[:, :], NEG).then_inc(s_cst, 1)
            pool.memset(ones[:, :], 1.0).then_inc(s_cst, 1)
            pool.memset(zeros[:, :, :], 0.0).then_inc(s_cst, 1)
            pool.wait_ge(s_cst, 5)
            pool.affine_select(out=ident[:, :], in_=ident[:, :], compare_op=ALU.not_equal, fill=1.0,
                               base=0, pattern=[[-1, P]], channel_multiplier=1).then_inc(s_cst, 1)
            pool.affine_select(out=mask[:, :], in_=mask[:, :], compare_op=ALU.is_ge, fill=NEG,
                               base=0, pattern=[[-1, P]], channel_multiplier=1).then_inc(s_cst, 1)
            pool.sem_inc(s_ad, RP)

            def step(h):
                for p, (qc, kp) in enumerate(PAIRS):
                    pr = probs[:, p % RP]
                    pool.wait_ge(s_ex, NP * h + p + 3)
                    if kp == 0:
                        pool.wait_ge(s_hv, 4 * h + qc + 1)
                        pool.tensor_tensor(acc[:, qc % 2], pr, zeros[:, :, :].to_broadcast([P, 2, QC]), ALU.add)\
                            .then_inc(s_ad, 1)
                        continue
                    pool.wait_ge(s_ad, NP * h + p + RP)
                    if diag(qc, 2 * kp) is None:
                        pool.tensor_tensor(acc[:, qc % 2], acc[:, qc % 2], pr, ALU.add).then_inc(s_ad, 1)
                    else:
                        for u in range(2):
                            o = off(qc, 2 * kp + u)
                            add = pool.tensor_tensor(acc[:, qc % 2, u, o:], acc[:, qc % 2, u, o:], pr[:, u, o:], ALU.add)
                        add.then_inc(s_ad, 1)

            with pool.Fori(0, H0 - 3, 2) as i:
                step(i)
                step(i + 1)
            step(H0 - 2)
            step(H0 - 1)

        @block.scalar
        def _(act):
            act.wait_ge(s_cstv, 5)
            act.sem_inc(s_ex, 2)
            act.sem_inc(s_oc, 1)

            def cast(h, j, c):
                act.wait_ge(s_qkp, 4 * h + c + 1)
                if not isinstance(h, int) or 4 * h + c >= 2:
                    act.wait_ge(s_lo, 4 * h + c - 1)
                if not isinstance(h, int) or h >= 1:
                    act.wait_ge(s_qkd[1 - j], 48 * (h + j))
                act.wait_ge(s_qb, h + 1)
                act.activation(qk32[:, c % 2, :], ps_x[:, :], ACT.Identity, bias=qkbias_head[:, j:j + 1],
                               scale=qkscale[:, 0:1])
                act.activation(qk_hi[:, c * QC:(c + 1) * QC], ps_x[:, :], ACT.Identity,
                               bias=qkbias_head[:, j:j + 1], scale=qkscale[:, 0:1]).then_inc(s_t32, 1)

            def exps(h, p):
                qc, kp = PAIRS[p]
                act.wait_ge(s_st, NP * h + p + 1)
                act.wait_ge(s_pv, NP * h + p + 1)
                act.wait_ge(s_ad, NP * h + p + 1)
                if diag(qc, 2 * kp) is None:
                    act.activation(probs[:, p % RP], ps_e[:, p % 2], ACT.Exp).then_inc(s_ex, 1)
                else:
                    for u in range(2):
                        o = off(qc, 2 * kp + u)
                        e = act.activation(probs[:, p % RP, u, o:], ps_e[:, p % 2, u, o:], ACT.Exp)
                    e.then_inc(s_ex, 1)

            def copy_pv(h, qc):
                act.wait_ge(s_pv, NP * h + LAST[qc] + 1 + RP)
                act.wait_ge(s_op, 4 * h + qc + 1)
                act.activation(pv_raw[:, qc % 2], ps_o[:, :], ACT.Copy).then_inc(s_oc, 1)

            for h in range(2):
                for c in range(4):
                    cast(h, h, c)

            def step(h, j, flags):
                fin, do_max, do_proj = flags
                for p in range(NP):
                    if p == 6 and do_max:
                        act.wait_ge(s_op, 4 * h + 2)
                    exps(h, p)
                    if p == 4 and do_proj:
                        load_wqk(act, h + 2, j)
                    if p == 6 and do_max:
                        load_wo(act, h + 1, 1 - j)
                    use = use_at(p, *flags)
                    if use and use[0] == "qk":
                        cast(h + 2, j, use[1])
                    if p == 0 and fin:
                        copy_pv(h - 1, 3)
                    if p - 1 in LAST:
                        copy_pv(h, LAST.index(p - 1))

            step(0, 0, FIRST)
            with act.Fori(1, H0 - 4, 2) as i:
                step(i, 1, FULL)
                step(i + 1, 0, FULL)
            step(H0 - 3, 1, FULL)
            step(H0 - 2, 0, NEXT_LAST)
            step(H0 - 1, 1, LAST_HEAD)
            copy_pv(H0 - 1, 3)

        @block.tensor
        def _(pe):
            pe.sem_inc(s_pv, RP)
            pe.sem_inc(s_sb, 1)
            pe.sem_inc(s_op, 2)
            pe.wait_ge(s_cst, 7)
            pe.wait_ge(s_ldx, 16)
            for n in range(4):
                if n >= 2:
                    pe.wait_ge(s_xtc, n - 1)
                for t in range(4):
                    tr = pe.transpose(ps_m[:, n % 2, t * P:(t + 1) * P], x_sb[:, 4 * n + t, :], ident[:, :])
                tr.then_inc(s_xt, 1)

            def v_product(n):
                t, c = n // 2, n % 2
                if n >= 4:
                    pe.wait_ge(s_vc, n - 3)
                pe.matmul(ps_e[:, (n % 4) // 2, n % 2], xt[:, t * P:(t + 1) * P],
                          wv[:, 8 * c:8 * c + 8, :].rearrange("m h d -> m (h d)"),
                          start=True, stop=True).then_inc(s_vp, 1)

            def proj(h, j, c, before):
                pe.wait_ge(s_xf, before + 1)
                if c == 0:
                    pe.wait_ge(s_wqk[j], 16 * (h - j) + 32)
                pe.matmul(ps_x[:, :], wqk[:, j, :], xt[:, c * QC:(c + 1) * QC], start=True, stop=True)\
                    .then_inc(s_qkp, 1)

            def max_chunk(h, j, n):
                qt, c = CH[n]
                if n == 0:
                    pe.wait_ge(s_qkd[j], 48 * (h - j) + 96)
                pe.wait_ge(s_mxr, NCH * h + n + 1)
                end = c == qt // 4
                w = P * (qt % 4 + 1) if end else QC
                mm = pe.matmul(ps_m[:, n % 2, 0:w], qq[:, j, qt * P:(qt + 1) * P], kk[:, j, c * QC:c * QC + w],
                               start=True, stop=not end)
                if end:
                    mm = pe.matmul(ps_m[:, n % 2, w - P:w], identb[:, :], mask[:, :], start=False, stop=True)
                mm.then_inc(s_mxp, 1)

            def max_transpose(h, g, before):
                pe.wait_ge(s_mhl, 4 * h + g + 1)
                pe.wait_ge(s_xf, before + 1)
                pe.transpose(ps_xh[0:8, 0:P], maxhl[:, :, :].rearrange("p r t -> p (r t)"), identh[:, :])\
                    .then_inc(s_mt, 1)

            def scores(h, j, p):
                qc, kp = PAIRS[p]
                if kp == 0:
                    pe.wait_ge(s_mrd[qc % 2], 64 * h + 32 * (qc // 2 + 1))
                pe.wait_ge(s_ex, NP * h + p + 1)
                for u in range(2):
                    kt = 2 * kp + u
                    o = off(qc, kt)
                    out = ps_e[:, p % 2, u]
                    keys = slice(kt * P, (kt + 1) * P)
                    queries = slice(qc * QC + o, (qc + 1) * QC)
                    jd = diag(qc, kt)
                    pe.matmul(out[:, o:], kk[:, j, keys], qq[:, j, queries], start=True, stop=False)
                    mm = pe.matmul(out[:, o:], km[0:D0 + 2, j, keys], qm[0:D0 + 2, j, queries],
                                   start=False, stop=jd is None)
                    if jd is not None:
                        for b in range(o // P, jd):
                            pe.matmul(out[:, b * P:(b + 1) * P], allneg[:, :], identb[:, :], start=False, stop=False)
                        mm = pe.matmul(out[:, jd * P:(jd + 1) * P], mask[:, :], identb[:, :], start=False, stop=True)
                mm.then_inc(s_st, 1)

            def pv(h, j, p):
                qc, kp = PAIRS[p]
                pe.wait_ge(s_ex, NP * h + p + 3)
                if p == 0:
                    pe.wait_ge(s_vh, h + 1)
                if kp == 0:
                    pe.wait_ge(s_oc, 4 * h + qc + 1)
                for u in range(2):
                    kt = 2 * kp + u
                    o = off(qc, kt)
                    mm = pe.matmul(ps_o[D0 * u:D0 * u + D0, o:], v_head[:, j, kt, :], probs[:, p % RP, u, o:],
                                   start=kp == 0, stop=p in LAST, skip_group_check=True)
                mm.then_inc(s_pv, 1)

            def row_sums(h, qc, before):
                pe.wait_ge(s_hv, 4 * h + qc + 3)
                pe.wait_ge(s_xf, before + 1)
                for t in range(4):
                    mm = pe.matmul(ps_x[:, t:t + 1], accsum[:, t * P:(t + 1) * P], ones[:, :], start=True, stop=True)
                mm.then_inc(s_sb, 1)

            def out_product(h, j, qc, before):
                if qc == 0:
                    pe.wait_ge(s_wo[j], 16 * (h - j) + 32)
                pe.wait_ge(s_oc, 4 * h + qc + 2)
                pe.wait_ge(s_xf, before + 1)
                for t in range(4):
                    mm = pe.matmul(ps_x[:, t * P:(t + 1) * P], pv_raw[:, qc % 2, t * P:(t + 1) * P], wo2[:, j, :],
                                   start=True, stop=True)
                mm.then_inc(s_op, 1)

            pe.wait_ge(s_ld, 80)
            pe.wait_ge(s_xtc, 4)
            for h in range(2):
                for c in range(4):
                    n = 4 * h + c
                    proj(h, h, c, n)
                    v_product(2 * n)
                    v_product(2 * n + 1)
            pe.wait_ge(s_cstv, 5)
            g = 0
            for n in range(NCH):
                max_chunk(0, 0, n)
                if 16 + n < 2 * NT:
                    v_product(16 + n)
                if n + 1 == GEND[g]:
                    max_transpose(0, g, 8 + g)
                    g += 1

            def step(h, j, flags):
                fin, do_max, do_proj = flags
                for p in range(NP):
                    scores(h, j, p)
                    chunks = list(range(*SLOT_CH[p])) if p in SLOT_CH and do_max else []
                    for n in chunks[:1]:
                        max_chunk(h + 1, 1 - j, n)
                    use = use_at(p, *flags)
                    if use:
                        kind, g, ahead = use
                        before = uses_before(h, flags, p)
                        if kind == "mt":
                            max_transpose(h + ahead, g, before)
                        elif kind == "sb":
                            row_sums(h + ahead, g, before)
                        elif kind == "op":
                            out_product(h + ahead, j if ahead == 0 else 1 - j, g, before)
                        else:
                            proj(h + 2, j, g, before)
                    for n in chunks[1:2]:
                        max_chunk(h + 1, 1 - j, n)
                    if p >= 1:
                        pv(h, j, p - 1)
                    elif fin:
                        pv(h - 1, 1 - j, NP - 1)
                    for n in chunks[2:]:
                        max_chunk(h + 1, 1 - j, n)

            pe.wait_ge(s_vc, 2 * NT)
            step(0, 0, FIRST)
            with pe.Fori(1, H0 - 4, 2) as i:
                step(i, 1, FULL)
                step(i + 1, 0, FULL)
            step(H0 - 3, 1, FULL)
            step(H0 - 2, 0, NEXT_LAST)
            step(H0 - 1, 1, LAST_HEAD)
            pv(H0 - 1, 1, NP - 1)
            row_sums(H0 - 1, 3, END_USES)
            out_product(H0 - 1, 1, 3, END_USES + 1)

        @block.vector
        def _(dve):
            dve.memset(qkscale[0:D0, :], 1.0 / math.sqrt(D0)).then_inc(s_dv, 1)
            dve.memset(qkscale[D0:P, :], 1.0).then_inc(s_dv, 1)
            dve.wait_ge(s_dv, 2)
            dve.wait_ge(s_ld, 80)
            dve.tensor_scalar(qkbias[:, :], qkbias[:, :], qkscale[:, 0:1], None, ALU.mult).then_inc(s_cstv, 1)
            dve.wait_ge(s_cstv, 1)
            for h in range(2):
                dve.tensor_copy(qkbias_head[:, h:h + 1], qkbias[:, h:h + 1]).then_inc(s_qb, 1)
            dve.wait_ge(s_cst, 7)
            dve.tensor_copy(identb[:, :], ident[:, :]).then_inc(s_cstv, 1)
            dve.tensor_copy(identh[:, :], ident[:, :]).then_inc(s_cstv, 1)
            dve.memset(km[D0:D0 + 2, :, :], -1.0).then_inc(s_cstv, 1)
            for n in range(4):
                dve.wait_ge(s_xt, n + 1)
                dve.tensor_copy(xt[:, n * QC:(n + 1) * QC], ps_m[:, n % 2]).then_inc(s_xtc, 1)
            dve.sem_inc(s_mxr, 2)
            dve.sem_inc(s_xf, 1)
            dve.sem_inc(s_hv, 2)
            dve.wait_ge(s_xtc, 4)
            dve.tensor_tensor(y_tok[:, :, :], x_sb[:, :, :], obias[:, :, :].to_broadcast([P, NT, P]), ALU.add)\
                .then_inc(s_cstv, 1)

            def v_out(n):
                t, c = n // 2, n % 2
                dve.wait_ge(s_vp, n + 1)
                dve.tensor_tensor(v_all[:, t, c * QC:(c + 1) * QC], ps_e[:, (n % 4) // 2, n % 2],
                                  vbias[:, c * QC:(c + 1) * QC], ALU.add).then_inc(s_vc, 1)

            def low(h, c):
                dve.wait_ge(s_t32, 4 * h + c + 1)
                dve.sem_inc(s_xf, 1)
                cols = slice(c * QC, (c + 1) * QC)
                dve.tensor_tensor(qk_lo[:, cols], qk32[:, c % 2, :], qk_hi[:, cols], ALU.subtract).then_inc(s_lo, 1)

            def take_max(h, n):
                qt, c = CH[n]
                w = P * (qt % 4 + 1) if c == qt // 4 else QC
                dve.wait_ge(s_mxp, NCH * h + n + 1)
                dve.reduce_max(maxpart[:, qt, c:c + 1], ps_m[:, n % 2, 0:w], AX.X).then_inc(s_mxr, 1)

            def split_max(h, g):
                dve.wait_ge(s_mxr, NCH * h + GEND[g] + 2)
                dve.wait_ge(s_mt, 4 * h + g)
                dve.reduce_max(rowmax[:, :], maxpart[:, 4 * g:4 * g + 4, 0:g + 1], AX.X).then_inc(s_dv, 1)
                dve.wait_ge(s_dv, 8 * h + 2 * g + 3)
                dve.tensor_copy(maxhl[:, 0, :], rowmax[:, :]).then_inc(s_dv, 1)
                dve.wait_ge(s_dv, 8 * h + 2 * g + 4)
                dve.tensor_tensor(maxhl[:, 1, :], rowmax[:, :], maxhl[:, 0, :], ALU.subtract).then_inc(s_mhl, 1)

            def max_out(h, g):
                dve.wait_ge(s_mt, 4 * h + g + 1)
                if not isinstance(h, int) or 4 * h + g >= 2:
                    dve.wait_ge(s_mrd[g % 2], 64 * h + 32 * (g // 2))
                dve.tensor_copy(maxrow[:, g % 2, :], ps_xh[0:8, 0:P]).then_inc(s_mc, 1)
                dve.wait_ge(s_mc, 4 * h + g + 1)
                dve.sem_inc(s_xf, 1)

            def add_halves(h, qc):
                dve.wait_ge(s_ad, NP * h + LAST[qc] + 1 + RP)
                dve.wait_ge(s_sb, 4 * h + qc + 1)
                dve.tensor_tensor(accsum[:, :], acc[:, qc % 2, 0], acc[:, qc % 2, 1], ALU.add).then_inc(s_hv, 1)

            def invert_sums(h, qc):
                dve.wait_ge(s_sb, 4 * h + qc + 2)
                dve.reciprocal(rden[:, :], ps_x[:, 0:4]).then_inc(s_rd, 1)
                dve.wait_ge(s_rd, 4 * h + qc + 1)
                dve.sem_inc(s_xf, 1)

            def add_out(h, qc):
                dve.wait_ge(s_op, 4 * h + qc + 3)
                for t in range(4):
                    add = dve.scalar_tensor_tensor(y_tok[:, 4 * qc + t, :], ps_x[:, t * P:(t + 1) * P],
                                                   rden[:, t:t + 1], y_tok[:, 4 * qc + t, :], ALU.mult, ALU.add)
                add.then_inc(s_ac, 1)
                dve.wait_ge(s_ac, 4 * h + qc + 1)
                dve.sem_inc(s_xf, 1)

            for h in range(2):
                for c in range(4):
                    low(h, c)
                    v_out(2 * (4 * h + c))
                    v_out(2 * (4 * h + c) + 1)
            g = 0
            for n in range(NCH):
                take_max(0, n)
                if 16 + n < 2 * NT:
                    v_out(16 + n)
                if n == 2 * NT - 16:
                    dve.wait_ge(s_vc, 2 * NT)
                    dve.tensor_copy(v_head[:, 0], v_all[:, :, 0:D0]).then_inc(s_vh, 1)
                if n + 1 == GEND[g]:
                    split_max(0, g)
                    max_out(0, g)
                    g += 1

            def step(h, j, flags):
                fin, do_max, do_proj = flags
                if do_proj:
                    dve.wait_ge(s_t32, 4 * h + 4)
                    dve.tensor_copy(qkbias_head[:, j:j + 1], qkbias[:, bass.ds(h + 2, 1)]).then_inc(s_qb, 1)
                for p in range(NP):
                    use = use_at(p - 1, *flags)
                    if use:
                        kind, g, ahead = use
                        if kind == "mt":
                            max_out(h + ahead, g)
                        elif kind == "sb":
                            invert_sums(h + ahead, g)
                        elif kind == "op":
                            add_out(h + ahead, g)
                        else:
                            low(h + 2, g)
                    if p in SLOT_CH and do_max:
                        for n in range(*SLOT_CH[p]):
                            take_max(h + 1, n)
                    use = use_at(p + 1, *flags)
                    if use and use[0] == "mt":
                        split_max(h + use[2], use[1])
                    if use and use[0] == "sb":
                        add_halves(h + use[2], use[1])
                    if p == 5 and do_max:
                        dve.wait_ge(s_pv, NP * h + RP)
                        dve.tensor_copy(v_head[:, 1 - j], v_all[:, :, bass.ds((h + 1) * D0, D0)]).then_inc(s_vh, 1)

            step(0, 0, FIRST)
            with dve.Fori(1, H0 - 4, 2) as i:
                step(i, 1, FULL)
                step(i + 1, 0, FULL)
            step(H0 - 3, 1, FULL)
            step(H0 - 2, 0, NEXT_LAST)
            step(H0 - 1, 1, LAST_HEAD)
            add_halves(H0 - 1, 3)
            invert_sums(H0 - 1, 3)
            add_out(H0 - 1, 3)
    norm_block(nc, "n0", yt, x_sb, xt, ident, tokens_first=True)

    with ExitStack() as ctx:
        def sb(name, shape, dt):
            return ctx.enter_context(nc.sbuf_tensor(name, shape, dt))

        def sem(name):
            return ctx.enter_context(nc.semaphore(name))

        NH = HID // P
        LAYERS = (("w1", NH, 1), ("w2", NH, 1), ("h1", NH, NH), ("h2", NH, NH), ("w3", 1, NH))
        raw = {n: sb(f"raw_{n}", [P, o, i * P], F32) for n, o, i in LAYERS}
        wt = {n: sb(f"wt_{n}", [P, i, o * P], F32) for n, o, i in LAYERS}
        sc = {n: sb(f"sc_{n}", [P, o], F32) for n, o, i in LAYERS}
        act_a = sb("act_a", [P, NH, S], F32)
        act_b = sb("act_b", [P, NH, S], F32)
        gate = sb("gate", [P, 4, QC], F32)
        ps = [ctx.enter_context(nc.psum_tensor(f"ps_f{n}", [P, QC], F32)) for n in range(8)]

        s_w = {n: sem(f"s_w_{n}") for n, _, _ in LAYERS}
        s_tp = sem("s_tp")
        s_tc = sem("s_tc")
        s_gp = sem("s_gp")
        s_up = sem("s_up")
        s_ga = sem("s_ga")
        s_gu = sem("s_gu")
        s_hp = sem("s_hp")
        s_ha = sem("s_ha")
        s_op = sem("s_op3")
        s_oy = sem("s_oy3")

        BLOCKS = [(n, o, i) for n, no, ni in LAYERS for o in range(no) for i in range(ni)]
        GROUPS = [BLOCKS[b:b + 4] for b in range(0, len(BLOCKS), 4)]
        block = ctx.enter_context(nc.Block())

        @block.sync
        def _(sp):
            with nc.allow_non_contiguous_dma(reason="small scale columns"):
                for n, no, ni in LAYERS:
                    sp.dma_start(raw[n][:, :, :], a[f"L0_ffn_{n}_w"].rearrange("(t p) i -> p t i", p=P))\
                        .then_inc(s_w[n], 16)
                    sp.dma_start(sc[n][:, :], a[f"L0_ffn_{n}_s"].rearrange("(t p) -> p t", p=P)).then_inc(s_w[n], 16)

        @block.tensor
        def _(pe):
            seen = set()
            for g, group in enumerate(GROUPS):
                if g >= 2:
                    pe.wait_ge(s_tc, g - 1)
                for b, (n, o, i) in enumerate(group):
                    if n not in seen:
                        pe.wait_ge(s_w[n], 32)
                        seen.add(n)
                    tr = pe.transpose(ps[g % 2][:, b * P:(b + 1) * P], raw[n][:, o, i * P:(i + 1) * P], ident[:, :])
                tr.then_inc(s_tp, 1)
            pe.wait_ge(s_tc, len(GROUPS))
            for n in range(NQ * NH):
                c, o = divmod(n, NH)
                if n >= 4:
                    pe.wait_ge(s_gu, n - 3)
                cols = slice(c * QC, (c + 1) * QC)
                pe.matmul(ps[n % 4][:, :], wt["w1"][:, 0, o * P:(o + 1) * P], xt[:, cols], start=True, stop=True)\
                    .then_inc(s_gp, 1)
                pe.matmul(ps[4 + n % 4][:, :], wt["w2"][:, 0, o * P:(o + 1) * P], xt[:, cols], start=True, stop=True)\
                    .then_inc(s_up, 1)
            pe.wait_ge(s_gu, NQ * NH)

            def hidden(name, src, k):
                for n in range(NQ * NH):
                    c, o = divmod(n, NH)
                    m = NQ * NH * k + n
                    if k == 1:
                        pe.wait_ge(s_ha, NH * (c + 1))
                    if m >= 8:
                        pe.wait_ge(s_ha, m - 7)
                    for i in range(NH):
                        mm = pe.matmul(ps[m % 8][:, :], wt[name][:, i, o * P:(o + 1) * P],
                                       src[:, i, c * QC:(c + 1) * QC], start=i == 0, stop=i == NH - 1)
                    mm.then_inc(s_hp, 1)

            hidden("h1", act_a, 0)
            hidden("h2", act_b, 1)
            for c in range(NQ):
                pe.wait_ge(s_ha, max(NQ * NH + NH * (c + 1), 2 * NQ * NH - 7 + c))
                for i in range(NH):
                    mm = pe.matmul(ps[c][:, :], wt["w3"][:, i, :], act_a[:, i, c * QC:(c + 1) * QC],
                                   start=i == 0, stop=i == NH - 1)
                mm.then_inc(s_op, 1)

        @block.scalar
        def _(act):
            act.wait_ge(s_w["w1"], 32)
            for n in range(NQ * NH):
                act.wait_ge(s_gp, n + 1)
                if n >= 4:
                    act.wait_ge(s_gu, n - 3)
                act.activation(gate[:, n % 4, :], ps[n % 4][:, :], ACT.Silu, scale=sc["w1"][:, n % NH:n % NH + 1])\
                    .then_inc(s_ga, 1)
            for k, (name, dst) in enumerate((("h1", act_b), ("h2", act_a))):
                act.wait_ge(s_w[name], 32)
                for n in range(NQ * NH):
                    c, o = divmod(n, NH)
                    m = NQ * NH * k + n
                    act.wait_ge(s_hp, m + 1)
                    if k == 1 and o == 0:
                        act.wait_ge(s_hp, NH * (c + 1))
                    act.activation(dst[:, o, c * QC:(c + 1) * QC], ps[m % 8][:, :], ACT.Gelu,
                                   scale=sc[name][:, o:o + 1]).then_inc(s_ha, 1)

        @block.vector
        def _(dve):
            for g, group in enumerate(GROUPS):
                dve.wait_ge(s_tp, g + 1)
                for b, (n, o, i) in enumerate(group):
                    ins = dve.tensor_copy(wt[n][:, i, o * P:(o + 1) * P], ps[g % 2][:, b * P:(b + 1) * P])
                ins.then_inc(s_tc, 1)
            dve.wait_ge(s_w["w2"], 32)
            dve.wait_ge(s_w["w3"], 32)
            for n in range(NQ * NH):
                c, o = divmod(n, NH)
                dve.wait_ge(s_up, n + 1)
                dve.wait_ge(s_ga, n + 1)
                dve.scalar_tensor_tensor(act_a[:, o, c * QC:(c + 1) * QC], ps[4 + n % 4][:, :],
                                         sc["w2"][:, o:o + 1], gate[:, n % 4, :], ALU.mult, ALU.mult).then_inc(s_gu, 1)
            for c in range(NQ):
                dve.wait_ge(s_op, c + 1)
                cols = slice(c * QC, (c + 1) * QC)
                dve.scalar_tensor_tensor(yt[:, cols], ps[c][:, :], sc["w3"][:, 0:1], xt[:, cols],
                                         ALU.mult, ALU.add).then_inc(s_oy, 1)
            dve.wait_ge(s_oy, NQ)

    norm_block(nc, "n1", yt, x_sb, xt, ident)

    NC = 4
    KB = S // NC
    R_A, R_W1, R_W0, R_M, R_END = 9 * D1, 9 * D1 + 6, 9 * D1 + 9, 9 * D1 + 12, 9 * D1 + 14
    GR = R_M - R_A
    CH1 = NC * H1
    qd = nc.dram_tensor("q_rows", (H1, R_A, S), BF16, kind="Internal").ap()
    kd = nc.dram_tensor("k_rows", (H1, R_A, S), BF16, kind="Internal").ap()
    gd = nc.dram_tensor("g_rows", (H1, GR, NC, S), BF16, kind="Internal").ap()

    l1 = ExitStack()
    v1 = l1.enter_context(nc.sbuf_tensor("v1", [P, NT, DM], F32))
    krows = l1.enter_context(nc.sbuf_tensor("krows", [P, 2, S], BF16))

    with ExitStack() as ctx:
        def sb(name, shape, dt):
            return ctx.enter_context(nc.sbuf_tensor(name, shape, dt))

        def sem(name):
            return ctx.enter_context(nc.semaphore(name))

        w1 = {n: sb(f"l1_{n}", [P, DM], F32) for n in ("wq", "wk", "wv", "wfq", "wfg")}
        col = {n: sb(f"l1_{n}", [P, 1], F32) for n in ("bq", "bk", "bfq", "bfg", "up", "uz")}
        bv = sb("l1_bv", [P, DM], F32)
        mq = sb("mq", [P, S], F32)
        mk = sb("mk", [P, S], F32)
        qs = yt
        rest = x_sb[:, :, :].rearrange("p t d -> p (t d)")
        parts = {n: sb(f"parts_{n}", [P, 3, S], BF16) for n in "qk"}
        gparts = {n: sb(f"parts_{n}", [CH1, 3, S], BF16) for n in ("a", "w1", "w0")}
        cgate = sb("cgate", [P, S], F32)
        blk = sb("blk", [P, NC, H1], F32)
        ublk = sb("ublk", [P, NC, H1], F32)
        zblk = sb("zblk", [P, NC, H1], F32)
        sp_ = sb("sig_p", [CH1, S], F32)
        sz = sb("sig_z", [CH1, S], F32)
        na = sb("na", [CH1, S], F32)
        uu = sb("uu", [CH1, S], F32)
        f1 = sb("f1", [CH1, S], F32)
        glo = sb("glo", [P, 1], F32)
        cbias = sb("cbias", [P, 1], F32)
        centre_row = sb("centre_row", [1, CH1], F32)
        centre = sb("centre", [CH1, 1], F32)
        dj = sb("dj", [1, S], F32)
        dj2 = sb("dj2", [1, S], F32)
        crow = sb("crow", [1, 5, S], BF16)
        ps = [ctx.enter_context(nc.psum_tensor(f"ps_p{n}", [P, QC], F32)) for n in range(8)]

        s_w = sem("s_w")
        s_i = sem("s_i")
        s_ctr = sem("s_ctr")
        s_qp = sem("s_qp")
        s_qa = sem("s_qa")
        s_va = sem("s_va")
        s_bl = sem("s_bl")
        s_gl = sem("s_gl")
        s_gp = sem("s_gp")
        s_cb = sem("s_cb")
        s_cp = sem("s_cp")
        s_ca = sem("s_ca")
        s_pp = sem("s_pp")
        s_pa = sem("s_pa")
        s_qs = sem("s_qs")
        s_pq = sem("s_pq")
        s_pt = sem("s_pt")
        s_pd = sem("s_pd")
        s_cr = sem("s_cr")
        s_dr = sem("s_dr")
        s_dv = sem("s_dv")
        block = ctx.enter_context(nc.Block())

        @block.sync
        def _(sp):
            n_w = 0
            for n in ("wq", "wk", "wv", "wfq", "wfg"):
                sp.dma_start(w1[n][:, :], a[f"L1_attn_{n}"]).then_inc(s_w, 16)
                n_w += 1
            with nc.allow_non_contiguous_dma(reason="small columns"):
                for n in ("bq", "bk", "bfq", "bfg"):
                    sp.dma_start(col[n][:, :], a[f"L1_attn_{n}"].rearrange("(m a) -> m a", a=1)).then_inc(s_w, 16)
                    n_w += 1
                for n in ("up", "uz"):
                    sp.dma_start(col[n][:, :], a[f"L1_attn_{n}"].rearrange("h a d -> (h d) a")).then_inc(s_w, 16)
                    n_w += 1
            sp.dma_start(bv[:, :], a["L1_attn_bv"].rearrange("(a n) -> a n", a=1).to_broadcast([P, DM]))\
                .then_inc(s_w, 16)
            assert n_w + 1 == 12
            sp.wait_ge(s_i, 4)
            with nc.allow_non_contiguous_dma(reason="a small row into a column"):
                sp.dma_start(centre[:, :], centre_row[0:1, :]).then_inc(s_ctr, 16)
            sp.wait_ge(s_cr, 5)
            n_d = 0
            for j in range(2):
                for r in range(R_END - R_A):
                    src = r % 2 if r < 6 else 2 if r < 9 else 3 if r < 12 else 4
                    sp.dma_start(krows[R_A + r:R_A + r + 1, j, :], crow[0:1, src, :]).then_inc(s_dr, 16)
                    n_d += 1
            for n, dst, split_done in (("k", kd, s_pt), ("q", qd, s_pq)):
                sp.wait_ge(split_done, 1)
                for i in range(3):
                    for jj in range(3):
                        row = D1 * (3 * i + jj)
                        sp.dma_start(dst[:, row:row + D1, :], parts[n][:, i if n == "q" else jj, :]).then_inc(s_dr, 16)
                        n_d += 1
            for m, (n, row, rep) in enumerate((("a", 0, 2), ("w1", 6, 1), ("w0", 9, 1))):
                sp.wait_ge(s_pt, m + 2)
                for i in range(3):
                    for r in range(rep):
                        sp.dma_start(gd[:, row + rep * i + r].rearrange("h c s -> c h s"), gparts[n][:, i, :])\
                            .then_inc(s_dr, 16)
                        n_d += 1
            sp.wait_ge(s_dr, 16 * n_d)

        @block.gpsimd
        def _(pool):
            pool.memset(blk[:, :, :], 1.0).then_inc(s_i, 1)
            pool.iota(centre_row[:, :], pattern=[[KB, NC], [0, H1]], base=KB // 2, channel_multiplier=0,
                      allow_small_or_imprecise_dtypes=True).then_inc(s_i, 1)
            pool.iota(dj[:, :], pattern=[[0, NC], [1, KB]], base=-(KB // 2), channel_multiplier=0,
                      allow_small_or_imprecise_dtypes=True).then_inc(s_i, 1)
            pool.wait_ge(s_i, 3)
            pool.affine_select(out=blk[:, :, :], in_=blk[:, :, :], compare_op=ALU.is_ge, fill=0.0,
                               base=0, pattern=[[0, NC], [-D1, H1]], channel_multiplier=1).then_inc(s_i, 1)
            pool.wait_ge(s_i, 4)
            pool.affine_select(out=blk[:, :, :], in_=blk[:, :, :], compare_op=ALU.is_ge, fill=0.0,
                               base=D1 - 1, pattern=[[0, NC], [D1, H1]], channel_multiplier=-1).then_inc(s_i, 1)
            pool.wait_ge(s_qs, 1)
            pool.tensor_copy(parts["q"][:, 0, :], qs[:, :]).then_inc(s_pd, 1)
            pool.wait_ge(s_pd, 1)
            pool.tensor_tensor(qs[:, :], qs[:, :], parts["q"][:, 0, :], ALU.subtract).then_inc(s_pd, 1)
            pool.wait_ge(s_pd, 2)
            pool.tensor_copy(parts["q"][:, 1, :], qs[:, :]).then_inc(s_pd, 1)
            pool.wait_ge(s_pd, 3)
            pool.tensor_tensor(parts["q"][:, 2, :], qs[:, :], parts["q"][:, 1, :], ALU.subtract).then_inc(s_pq, 1)

        @block.tensor
        def _(pe):
            pe.wait_ge(s_w, 192)
            for n in range(8):
                c = n % 4
                pe.matmul(ps[n][:, :], w1["wq" if n < 4 else "wk"][:, :], xt[:, c * QC:(c + 1) * QC],
                          start=True, stop=True).then_inc(s_qp, 1)
            pe.wait_ge(s_qa, 4)
            for g in range(4):
                for t in range(4):
                    n = 4 * g + t
                    mm = pe.matmul(ps[g][:, t * P:(t + 1) * P], xt[:, n * P:(n + 1) * P], w1["wv"][:, :],
                                   start=True, stop=True)
                mm.then_inc(s_qp, 1)
            pe.wait_ge(s_gl, 1)
            pe.wait_ge(s_qa, 8)
            pe.matmul(ps[4][:, 0:1], w1["wfg"][:, :], glo[:, :], start=True, stop=True).then_inc(s_gp, 1)
            pe.wait_ge(s_va, 4)
            for c in range(4):
                pe.matmul(ps[c][:, :], w1["wfq"][:, :], mq[:, c * QC:(c + 1) * QC], start=True, stop=True)\
                    .then_inc(s_cp, 1)
            pe.wait_ge(s_bl, 2)
            pe.wait_ge(s_cb, 1)
            for c in range(4):
                pe.wait_ge(s_ca, c + 1)
                if c >= 2:
                    pe.wait_ge(s_pa, 2 * (c - 2) + 2)
                for m, u in enumerate((ublk, zblk)):
                    pe.matmul(ps[4 + 2 * (c % 2) + m][0:CH1, :], u[:, :, :].rearrange("p c h -> p (c h)"),
                              cgate[:, c * QC:(c + 1) * QC], start=True, stop=True).then_inc(s_pp, 1)

        @block.scalar
        def _(act):
            act.wait_ge(s_w, 192)
            for n in range(8):
                c = n % 4
                act.wait_ge(s_qp, n + 1)
                act.activation((mq if n < 4 else mk)[:, c * QC:(c + 1) * QC], ps[n][:, :], ACT.Identity,
                               bias=col["bq" if n < 4 else "bk"][:, 0:1]).then_inc(s_qa, 1)
            act.wait_ge(s_cb, 1)
            for c in range(4):
                act.wait_ge(s_cp, c + 1)
                act.activation(cgate[:, c * QC:(c + 1) * QC], ps[c][:, :], ACT.Tanh, bias=cbias[:, 0:1])\
                    .then_inc(s_ca, 1)
            for c in range(4):
                for m, dst in enumerate((sp_, sz)):
                    act.wait_ge(s_pp, 2 * c + m + 1)
                    act.activation(dst[:, c * QC:(c + 1) * QC], ps[4 + 2 * (c % 2) + m][0:CH1, :], ACT.Sigmoid)\
                        .then_inc(s_pa, 1)

        @block.vector
        def _(dve):
            done = [0]

            def link(ins):
                done[0] += 1
                ins.then_inc(s_dv, 1)
                dve.wait_ge(s_dv, done[0])

            def split(src, dst, n):
                link(dve.tensor_copy(dst[:, 0, :], src))
                link(dve.tensor_tensor(rest[0:n, :], src, dst[:, 0, :], ALU.subtract))
                link(dve.tensor_copy(dst[:, 1, :], rest[0:n, :]))
                ins = dve.tensor_tensor(dst[:, 2, :], rest[0:n, :], dst[:, 1, :], ALU.subtract)
                ins.then_inc(s_pt, 1)
                dve.wait_ge(s_pt, splits.pop(0))

            splits = [1, 2, 3, 4]
            dve.memset(crow[0:1, 3, :], 1.0).then_inc(s_cr, 1)
            dve.memset(crow[0:1, 4, :], -1.0).then_inc(s_cr, 1)
            dve.wait_ge(s_i, 5)
            link(dve.tensor_tensor(dj2[:, :], dj[:, :], dj[:, :], ALU.mult))
            dve.tensor_copy(crow[0:1, 0, :], dj2[:, :]).then_inc(s_cr, 1)
            dve.tensor_copy(crow[0:1, 2, :], dj[:, :]).then_inc(s_cr, 1)
            dve.wait_ge(s_cr, 4)
            dve.tensor_tensor(crow[0:1, 1, :], dj2[:, :], crow[0:1, 0, :], ALU.subtract).then_inc(s_cr, 1)
            dve.wait_ge(s_w, 192)
            for dst, n in ((ublk, "up"), (zblk, "uz")):
                dve.tensor_scalar(dst[:, :, :], blk[:, :, :], col[n][:, 0:1], None, ALU.mult).then_inc(s_bl, 1)
            dve.wait_ge(s_qa, 4)
            dve.tensor_scalar(qs[:, :], mq[:, :], 1.0 / math.sqrt(D1), None, ALU.mult).then_inc(s_qs, 1)
            link(dve.reduce_sum(glo[:, :], mq[:, :], AX.X))
            dve.tensor_scalar(glo[:, :], glo[:, :], 1.0 / S, None, ALU.mult).then_inc(s_gl, 1)
            for g in range(4):
                dve.wait_ge(s_qp, 9 + g)
                for t in range(4):
                    ins = dve.tensor_tensor(v1[:, 4 * g + t, :], ps[g][:, t * P:(t + 1) * P], bv[:, :], ALU.add)
                ins.then_inc(s_va, 1)
            dve.wait_ge(s_gp, 1)
            link(dve.tensor_tensor(cbias[:, :], ps[4][:, 0:1], col["bfg"][:, :], ALU.add))
            dve.tensor_tensor(cbias[:, :], cbias[:, :], col["bfq"][:, :], ALU.add).then_inc(s_cb, 1)
            dve.wait_ge(s_qa, 8)
            split(mk[:, :], parts["k"], P)
            for c in range(4):
                cols = slice(c * QC, (c + 1) * QC)
                dve.wait_ge(s_pa, 2 * c + 2)
                link(dve.reciprocal(f1[:, cols], sz[:, cols]))
                link(dve.scalar_tensor_tensor(na[:, cols], f1[:, cols], -2.0 / (S * S), f1[:, cols], ALU.mult, ALU.mult))
            split(na[:, :], gparts["a"], CH1)
            dve.wait_ge(s_ctr, 16)
            link(dve.tensor_scalar(uu[:, :], sp_[:, :], float(S), centre[:, 0:1], ALU.mult, ALU.subtract))
            link(dve.scalar_tensor_tensor(f1[:, :], na[:, :], -2.0, uu[:, :], ALU.mult, ALU.mult))
            link(dve.scalar_tensor_tensor(uu[:, :], f1[:, :], -0.5, uu[:, :], ALU.mult, ALU.mult))
            split(f1[:, :], gparts["w1"], CH1)
            split(uu[:, :], gparts["w0"], CH1)

    ctxt = l1.enter_context(nc.sbuf_tensor("ctxt", [P, NT, DM], F32))
    with ExitStack() as ctx:
        def sb(name, shape, dt):
            return ctx.enter_context(nc.sbuf_tensor(name, shape, dt))

        def psum(name, shape, dt=F32):
            return ctx.enter_context(nc.psum_tensor(name, shape, dt))

        def sem(name):
            return ctx.enter_context(nc.semaphore(name))

        RP1 = 8
        CG = 4
        RING = 3
        qrows = sb("qrows", [P, 2, NC, S], BF16)
        v_head = sb("v1_head", [P, 2, NT, 32], F32)
        probs = sb("probs1", [P, RP1, 2, QC], F32)
        maxpart = sb("maxpart1", [P, NT, NC], F32)
        rowmax = sb("rowmax1", [P, 4], F32)
        maxhl = sb("maxhl1", [P, 2, 4], BF16)
        maxrow = sb("maxrow1", [8, 2, P], BF16)
        identb = sb("identb1", [P, P], BF16)
        sel = sb("sel", [P, 16], F32)
        pv_raw = sb("pv_raw1", [P, QC], F32)
        rden = sb("rden1", [P, 4, 1], F32)

        ps_e = psum("ps_e1", [P, 2, 2, QC])
        ps_o = psum("ps_o1", [P, QC])
        ps_r = psum("ps_r1", [P, RING, QC])

        s_q = [[sem(f"s_q{j}{c}") for c in range(NQ)] for j in range(2)]
        s_k = [sem(f"s_k{j}") for j in range(2)]
        s_cst = sem("s_cst1")
        s_cv = sem("s_cv1")
        s_rp = sem("s_rp1")
        s_mt = sem("s_mt1")
        s_rf = sem("s_rf1")
        s_mhl = sem("s_mhl1")
        s_mc = sem("s_mc1")
        s_mrd = [sem(f"s_mrd1{g}") for g in range(2)]
        s_st = sem("s_st1")
        s_ex = sem("s_ex1")
        s_pv = sem("s_pv1")
        s_oc = sem("s_oc1")
        s_vh = sem("s_vh1")
        s_fp = sem("s_fp1")
        s_rd = sem("s_rd1")
        s_fn = sem("s_fn1")
        s_dv = sem("s_dv1")

        MR = 16 * 2 * NC
        KP = NT // 2
        NP1 = NQ * KP
        NCH1 = NT * NC

        NTURN = NP1 // 2
        FN_AT = {5: 0, 9: 1, 13: 2}
        MT_AT = {6: 0, 10: 1, 14: 2}
        LATE_FN, LATE_MT = 1, 2

        def turn_uses(t, first, do_max):
            n = 4 * (t - 1)
            ch = [("max", n + k) for k in range(4)] if do_max and t >= 1 else [None] * 4
            extra = []
            if t in FN_AT:
                extra.append(("fn", FN_AT[t], 0))
            if t == LATE_FN and not first:
                extra.append(("fn", 3, -1))
            if t in MT_AT and do_max:
                extra.append(("mt", MT_AT[t], 1))
            if t == LATE_MT:
                extra.append(("mt", 3, 0))
            return ch, extra

        def ring_uses(first, do_max):
            out = []
            for t in range(NTURN):
                ch, extra = turn_uses(t, first, do_max)
                out += [c for c in ch[0:3] if c] + extra + [c for c in ch[3:] if c]
            if do_max:
                out += [("max", n) for n in range(4 * (NTURN - 1), NCH1)]
            return out

        BEFORE = [u for g in range(4) for u in [("max", n) for n in range(16 * g, 16 * g + 16)] + [("mt", g, 1)]][:-1]
        FULL = len(ring_uses(False, True))
        SHIFT = len(BEFORE) + len(ring_uses(True, True)) - FULL
        assert FULL % RING == 0

        def ring_base(h, first):
            return (len(BEFORE), len(BEFORE) % RING) if first else (SHIFT + FULL * h, SHIFT % RING)

        def load_q(eng, h, j, c):
            cols = slice(c * QC, (c + 1) * QC)
            eng.dma_start(qrows[0:R_A, j, :, cols],
                          qd[bass.ds(h, 1), :, cols].rearrange("a (r c) s -> (a r) c s", c=1)
                          .to_broadcast([R_A, NC, QC])).then_inc(s_q[j][c], 16)
            eng.dma_start(qrows[R_A:R_M, j, :, cols],
                          gd[bass.ds(h, 1), :, :, cols].rearrange("a r c s -> (a r) c s")).then_inc(s_q[j][c], 16)

        def load_k(eng, h, j):
            eng.dma_start(krows[0:R_A, j, :], kd[bass.ds(h, 1)].rearrange("a r s -> (a r) s")).then_inc(s_k[j], 16)

        block = ctx.enter_context(nc.Block())

        @block.sync
        def _(sp):
            load_k(sp, 0, 0)
            for h in range(2):
                if h:
                    load_k(sp, h, h)
                for c in range(NQ):
                    load_q(sp, h, h, c)

            def place_max(h, j, g):
                sp.wait_ge(s_mc, 4 * h + g + 1)
                for r in range(2):
                    for c in range(NC):
                        sp.dma_start(qrows[R_M + r:R_M + r + 1, j, c, g * QC:(g + 1) * QC],
                                     maxrow[4 * r:4 * r + 4, g % 2, :]).then_inc(s_mrd[g % 2], 16)

            with sp.Fori(0, H1 - 1, 2) as i:
                for j in range(2):
                    for g in range(4):
                        place_max(i + j, j, g)

        @block.gpsimd
        def _(pool):
            pool.memset(sel[:, :], 0.0).then_inc(s_cst, 1)
            pool.wait_ge(s_cst, 1)
            for g in range(CG):
                pool.affine_select(out=sel[:, :], in_=sel[:, :], compare_op=ALU.not_equal, fill=1.0,
                                   base=-32 * g, pattern=[[-1, 16]], channel_multiplier=1).then_inc(s_cst, 1)
                pool.wait_ge(s_cst, 2 + g)

        @block.scalar
        def _(act):
            act.sem_inc(s_ex, 2)
            act.sem_inc(s_oc, 1)

            def exps(h, p):
                act.wait_ge(s_st, NP1 * h + p + 1)
                act.wait_ge(s_pv, NP1 * h + p + 1)
                act.activation(probs[:, p % RP1], ps_e[:, p % 2], ACT.Exp).then_inc(s_ex, 1)

            def copy_pv(h, qc):
                act.wait_ge(s_pv, NP1 * h + KP * (qc + 1) + RP1)
                act.wait_ge(s_fp, 4 * h + qc + 1)
                act.activation(pv_raw[:, :], ps_o[:, :], ACT.Copy).then_inc(s_oc, 1)

            def step(h, j, first, more):
                for p in range(NP1):
                    exps(h, p)
                    if p in (8, 16, 24) and more:
                        load_q(act, h + 2, j, p // 8 - 1)
                    if p in (9, 17, 25):
                        copy_pv(h, p // 8 - 1)
                    if p == 1 and not first:
                        copy_pv(h - 1, 3)
                if more:
                    load_k(act, h + 2, j)
                    load_q(act, h + 2, j, 3)

            step(0, 0, True, True)
            with act.Fori(1, H1 - 4, 2) as i:
                step(i, 1, False, True)
                step(i + 1, 0, False, True)
            step(H1 - 3, 1, False, True)
            step(H1 - 2, 0, False, False)
            step(H1 - 1, 1, False, False)
            copy_pv(H1 - 1, 3)

        @block.tensor
        def _(pe):
            pe.sem_inc(s_pv, RP1)
            pe.sem_inc(s_fp, 1)

            def max_chunk(h, j, n, use, bank):
                qt, c = divmod(n, NC)
                if n == 0:
                    pe.wait_ge(s_k[j], 8 * (h - j) + 16)
                if n % (4 * NC) == 0:
                    pe.wait_ge(s_q[j][qt // 4], 16 * (h - j) + 32)
                pe.wait_ge(s_rf, use + 1)
                pe.matmul(ps_r[:, bank, :], qrows[0:R_M, j, c, qt * P:(qt + 1) * P],
                          krows[0:R_M, j, c * KB:(c + 1) * KB], start=True, stop=True).then_inc(s_rp, 1)

            def max_transpose(h, g, use, bank):
                pe.wait_ge(s_mhl, 4 * h + g + 1)
                pe.wait_ge(s_rf, use + 1)
                pe.transpose(ps_r[:, bank, :].bitcast(BF16)[0:8, 0:P], maxhl[:, :, :].rearrange("p r t -> p (r t)"),
                             identb[:, :]).then_inc(s_mt, 1)

            def scores(h, j, p):
                qc, kp = divmod(p, KP)
                if kp == 0:
                    pe.wait_ge(s_mrd[qc % 2], MR * (2 * h + qc // 2 + 1))
                pe.wait_ge(s_ex, NP1 * h + p + 1)
                for u in range(2):
                    kt = 2 * kp + u
                    mm = pe.matmul(ps_e[:, p % 2, u], krows[0:R_END, j, kt * P:(kt + 1) * P],
                                   qrows[0:R_END, j, kt * P // KB, qc * QC:(qc + 1) * QC], start=True, stop=True)
                mm.then_inc(s_st, 1)

            def pv(h, j, p):
                qc, kp = divmod(p, KP)
                pe.wait_ge(s_ex, NP1 * h + p + 4)
                if p == 0:
                    pe.wait_ge(s_vh, h + 1)
                if kp == 0:
                    pe.wait_ge(s_oc, 4 * h + qc + 1)
                for u in range(CG):
                    kt = 2 * kp + u
                    mm = pe.matmul(ps_o[32 * u:32 * u + 32, :], v_head[:, j, kt, :],
                                   probs[:, (p + u // 2) % RP1, u % 2], start=kp == 0, stop=kp == KP - 2,
                                   skip_group_check=True)
                mm.then_inc(s_pv, 2)

            def finish(h, qc, use, bank):
                pe.wait_ge(s_oc, 4 * h + qc + 2)
                pe.wait_ge(s_rf, use + 1)
                for t in range(4):
                    mm = pe.matmul(ps_r[:, bank, 16 * t:16 * t + 16], pv_raw[:, t * P:(t + 1) * P], sel[:, :],
                                   start=True, stop=True)
                mm.then_inc(s_fp, 1)

            pe.wait_ge(s_cst, 5)
            pe.wait_ge(s_cv, 2)
            for at, use in enumerate(BEFORE):
                if use[0] == "max":
                    max_chunk(0, 0, use[1], at, at % RING)
                else:
                    max_transpose(0, use[1], at, at % RING)

            def step(h, j, first, do_max):
                base, mod = ring_base(h, first)
                local = [0]

                def ring(use):
                    at, bank = base + local[0], (mod + local[0]) % RING
                    local[0] += 1
                    if use[0] == "max":
                        max_chunk(h + 1, 1 - j, use[1], at, bank)
                    elif use[0] == "mt":
                        max_transpose(h + use[2], use[1], at, bank)
                    else:
                        finish(h + use[2], use[1], at, bank)

                for t in range(NTURN):
                    ch, extra = turn_uses(t, first, do_max)
                    if ch[0]:
                        ring(ch[0])
                    scores(h, j, 2 * t)
                    if ch[1]:
                        ring(ch[1])
                    scores(h, j, 2 * t + 1)
                    if ch[2]:
                        ring(ch[2])
                    for use in extra:
                        ring(use)
                    if t >= 1:
                        pv(h, j, 2 * t - 2)
                    elif not first:
                        pv(h - 1, 1 - j, NP1 - 2)
                    if ch[3]:
                        ring(ch[3])
                if do_max:
                    for n in range(4 * (NTURN - 1), NCH1):
                        ring(("max", n))
                assert local[0] == len(ring_uses(first, do_max))

            step(0, 0, True, True)
            with pe.Fori(1, H1 - 4, 2) as i:
                step(i, 1, False, True)
                step(i + 1, 0, False, True)
            step(H1 - 3, 1, False, True)
            step(H1 - 2, 0, False, True)
            step(H1 - 1, 1, False, False)
            pv(H1 - 1, 1, NP1 - 2)
            finish(H1 - 1, 3, SHIFT + FULL * (H1 - 1) + len(ring_uses(False, False)),
                   (SHIFT + len(ring_uses(False, False))) % RING)

        @block.vector
        def _(dve):
            dve.tensor_copy(identb[:, :], ident[:, :]).then_inc(s_cv, 1)
            dve.memset(v_head[:, :, :, :], 0.0).then_inc(s_dv, 1)
            dve.wait_ge(s_dv, 1)
            dve.memset(v_head[:, :, :, D1:D1 + 1], 1.0).then_inc(s_cv, 1)
            dve.sem_inc(s_rf, RING)

            def take_max(h, n, bank):
                qt, c = divmod(n, NC)
                dve.wait_ge(s_rp, NCH1 * h + n + 1)
                dve.reduce_max(maxpart[:, qt, c:c + 1], ps_r[:, bank, :], AX.X).then_inc(s_rf, 1)

            def split_max(h, g, read):
                dve.wait_ge(s_rf, read)
                dve.reduce_max(rowmax[:, :], maxpart[:, 4 * g:4 * g + 4, :], AX.X).then_inc(s_dv, 1)
                dve.wait_ge(s_dv, 12 * h + 3 * g + 2)
                dve.tensor_scalar(rowmax[:, :], rowmax[:, :], HEADROOM, None, ALU.add).then_inc(s_dv, 1)
                dve.wait_ge(s_dv, 12 * h + 3 * g + 3)
                dve.tensor_copy(maxhl[:, 0, :], rowmax[:, :]).then_inc(s_dv, 1)
                dve.wait_ge(s_dv, 12 * h + 3 * g + 4)
                dve.tensor_tensor(maxhl[:, 1, :], rowmax[:, :], maxhl[:, 0, :], ALU.subtract).then_inc(s_mhl, 1)

            def max_out(h, g, bank):
                dve.wait_ge(s_mt, 4 * h + g + 1)
                if not isinstance(h, int) or 4 * h + g >= 2:
                    dve.wait_ge(s_mrd[g % 2], MR * (2 * h + g // 2))
                dve.tensor_copy(maxrow[:, g % 2, :], ps_r[:, bank, :].bitcast(BF16)[0:8, 0:P]).then_inc(s_mc, 1)
                dve.wait_ge(s_mc, 4 * h + g + 1)
                dve.sem_inc(s_rf, 1)

            def normalise(h, qc, bank):
                dve.wait_ge(s_fp, 4 * h + qc + 2)
                x = ps_r[:, bank, 0:64].rearrange("p (t c) -> p t c", c=16)
                dve.reciprocal(rden[:, :, :], x[:, :, D1:D1 + 1]).then_inc(s_rd, 1)
                dve.wait_ge(s_rd, 4 * h + qc + 1)
                dve.tensor_tensor(ctxt[:, 4 * qc:4 * qc + 4, bass.ds(D1 * h, D1)], x[:, :, 0:D1],
                                  rden[:, :, :].to_broadcast([P, 4, D1]), ALU.mult).then_inc(s_fn, 1)
                dve.wait_ge(s_fn, 4 * h + qc + 1)
                dve.sem_inc(s_rf, 1)

            def read_ring(h, j, uses, base, mod):
                for k, use in enumerate(uses):
                    bank = (mod + k) % RING
                    if use[0] == "max":
                        take_max(h, use[1], bank)
                        if use[1] % 16 == 15:
                            split_max(h, use[1] // 16, base + k + 1 + RING)
                    elif use[0] == "mt":
                        max_out(h - 1 + use[2], use[1], bank)
                    else:
                        normalise(h - 1 + use[2], use[1], bank)
                    if use == ("max", 20):
                        if not isinstance(h, int) or h >= 2:
                            dve.wait_ge(s_pv, NP1 * (h - 1) + RP1)
                        dve.tensor_copy(v_head[:, j, :, 0:D1], v1[:, :, bass.ds(h * D1, D1)]).then_inc(s_vh, 1)

            def step(h, j, first, do_max):
                base, mod = ring_base(h, first)
                read_ring(h + 1, 1 - j, ring_uses(first, do_max), base, mod)

            read_ring(0, 0, BEFORE, 0, 0)
            step(0, 0, True, True)
            with dve.Fori(1, H1 - 4, 2) as i:
                step(i, 1, False, True)
                step(i + 1, 0, False, True)
            step(H1 - 3, 1, False, True)
            step(H1 - 2, 0, False, True)
            step(H1 - 1, 1, False, False)
            normalise(H1 - 1, 3, (SHIFT + len(ring_uses(False, False))) % RING)

    with ExitStack() as ctx:
        def sem(name):
            return ctx.enter_context(nc.semaphore(name))

        wo = ctx.enter_context(nc.sbuf_tensor("l1_wo", [P, DM], F32))
        bo = ctx.enter_context(nc.sbuf_tensor("l1_bo", [P, 1], F32))
        xb = ctx.enter_context(nc.sbuf_tensor("x_bias", [P, S], F32))
        ct = ctx.enter_context(nc.sbuf_tensor("ct", [P, S], F32))
        ps = [ctx.enter_context(nc.psum_tensor(f"ps_wo{n}", [P, QC], F32)) for n in range(8)]
        s_w = sem("s_wo1")
        s_tp = sem("s_tp1")
        s_tc = sem("s_tc1")
        s_op = sem("s_op1")
        s_xb = sem("s_xb1")
        s_oy = sem("s_oy1")
        block = ctx.enter_context(nc.Block())

        @block.sync
        def _(sp):
            sp.dma_start(wo[:, :], a["L1_attn_wo"]).then_inc(s_w, 16)
            with nc.allow_non_contiguous_dma(reason="small column"):
                sp.dma_start(bo[:, :], a["L1_attn_bo"].rearrange("(m a) -> m a", a=1)).then_inc(s_w, 16)

        @block.tensor
        def _(pe):
            for g in range(4):
                for t in range(4):
                    tr = pe.transpose(ps[g][:, t * P:(t + 1) * P], ctxt[:, 4 * g + t, :], ident[:, :])
                tr.then_inc(s_tp, 1)
            pe.wait_ge(s_w, 32)
            for g in range(4):
                pe.wait_ge(s_tc, g + 1)
                pe.matmul(ps[4 + g][:, :], wo[:, :], ct[:, g * QC:(g + 1) * QC], start=True, stop=True)\
                    .then_inc(s_op, 1)

        @block.scalar
        def _(act):
            for g in range(4):
                act.wait_ge(s_tp, g + 1)
                act.activation(ct[:, g * QC:(g + 1) * QC], ps[g][:, :], ACT.Copy).then_inc(s_tc, 1)

        @block.vector
        def _(dve):
            dve.wait_ge(s_w, 32)
            dve.tensor_scalar(xb[:, :], xt[:, :], bo[:, 0:1], None, ALU.add).then_inc(s_xb, 1)
            dve.wait_ge(s_xb, 1)
            for g in range(4):
                cols = slice(g * QC, (g + 1) * QC)
                dve.wait_ge(s_op, g + 1)
                dve.tensor_tensor(yt[:, cols], ps[4 + g][:, :], xb[:, cols], ALU.add).then_inc(s_oy, 1)
            dve.wait_ge(s_oy, 4)

    l1.close()
    norm_block(nc, "n2", yt, x_sb, xt, ident)

    with ExitStack() as ctx:
        def sb(name, shape):
            return ctx.enter_context(nc.sbuf_tensor(name, shape, F32))

        def sem(name):
            return ctx.enter_context(nc.semaphore(name))

        RANK, DD = a["L1_ffn_lora_down"].shape
        UD = a["L1_ffn_lora_up"].shape[0]
        w_raw = sb("w_raw", [P, DM])
        w_t = sb("w_t", [P, DM])
        ua_raw = sb("ua_raw", [P, UD])
        ua_t = sb("ua_t", [UD, P])
        lu_raw = sb("lu_raw", [UD, RANK])
        lu_t = sb("lu_t", [RANK, UD])
        ld_raw = sb("ld_raw", [RANK, DD])
        ld_t = sb("ld_t", [DD, RANK])
        da = sb("da", [DD, DM])
        inner = sb("inner", [RANK, DM])
        outer = sb("outer", [UD, DM])
        bcol = sb("bcol", [P, 1])
        xb = sb("x_bias2", [P, S])
        ps = [ctx.enter_context(nc.psum_tensor(f"ps_l{n}", [P, QC], F32)) for n in range(8)]
        s_w = sem("s_w2")
        s_tp = sem("s_tp2")
        s_tc = sem("s_tc2")
        s_lp = sem("s_lp2")
        s_lc = sem("s_lc2")
        s_op = sem("s_op2")
        s_xb = sem("s_xb2")
        s_oy = sem("s_oy2")
        block = ctx.enter_context(nc.Block())
        TURN = ((w_raw, w_t, P, DM), (ua_raw, ua_t, P, UD), (lu_raw, lu_t, UD, RANK), (ld_raw, ld_t, RANK, DD))

        @block.sync
        def _(sp):
            for n, dst in (("W", w_raw), ("up_aux", ua_raw), ("lora_up", lu_raw), ("lora_down", ld_raw),
                           ("down_aux", da)):
                sp.dma_start(dst[:, :], a[f"L1_ffn_{n}"]).then_inc(s_w, 16)
            with nc.allow_non_contiguous_dma(reason="small column"):
                sp.dma_start(bcol[:, :], a["L1_ffn_b"].rearrange("(m a) -> m a", a=1)).then_inc(s_w, 16)

        @block.tensor
        def _(pe):
            pe.wait_ge(s_w, 96)
            for n, (raw, _, rows, cols) in enumerate(TURN):
                pe.transpose(ps[n][0:cols, 0:rows], raw[:, :], ident[0:rows, 0:rows]).then_inc(s_tp, 1)
            pe.wait_ge(s_tc, 4)
            pe.matmul(ps[4][0:RANK, 0:DM], ld_t[:, :], da[:, :], start=True, stop=True).then_inc(s_lp, 1)
            pe.wait_ge(s_lc, 1)
            pe.matmul(ps[5][0:UD, 0:DM], lu_t[:, :], inner[:, :], start=True, stop=True).then_inc(s_lp, 1)
            pe.wait_ge(s_lc, 2)
            pe.matmul(ps[6][:, 0:P], outer[:, :], ua_t[:, :], start=True, stop=True).then_inc(s_lp, 1)
            pe.wait_ge(s_lc, 3)
            for g in range(4):
                pe.matmul(ps[g][:, :], w_t[:, :], xt[:, g * QC:(g + 1) * QC], start=True, stop=True)\
                    .then_inc(s_op, 1)

        @block.vector
        def _(dve):
            dve.wait_ge(s_w, 96)
            dve.tensor_scalar(xb[:, :], xt[:, :], bcol[:, 0:1], None, ALU.add).then_inc(s_xb, 1)
            for n, (_, dst, rows, cols) in enumerate(TURN):
                dve.wait_ge(s_tp, n + 1)
                dve.tensor_copy(dst[:, :], ps[n][0:cols, 0:rows]).then_inc(s_tc, 1)
            for n, (dst, rows) in enumerate(((inner, RANK), (outer, UD))):
                dve.wait_ge(s_lp, n + 1)
                dve.tensor_copy(dst[:, :], ps[4 + n][0:rows, 0:DM]).then_inc(s_lc, 1)
            dve.wait_ge(s_lp, 3)
            dve.wait_ge(s_tc, 4)
            dve.tensor_tensor(w_t[:, :], w_t[:, :], ps[6][:, 0:P], ALU.add).then_inc(s_lc, 1)
            dve.wait_ge(s_xb, 1)
            for g in range(4):
                cols = slice(g * QC, (g + 1) * QC)
                dve.wait_ge(s_op, g + 1)
                dve.tensor_tensor(yt[:, cols], ps[g][:, :], xb[:, cols], ALU.add).then_inc(s_oy, 1)
            dve.wait_ge(s_oy, 4)

    norm_block(nc, "n3", yt, x_sb, xt, ident, out_dram)
    persist.close()


def kernel(**inputs):
    import concourse.bacc as _bacc
    from concourse.bass_utils import run_bass_kernel_spmd as _run

    nc = _bacc.Bacc("TRN2", target_bir_lowering=False, num_devices=1)
    arrays, args = {}, {}
    for name in sorted(inputs):
        v = np.ascontiguousarray(inputs[name])
        arrays[f"in_{name}"] = v
        args[name] = nc.dram_tensor(f"in_{name}", v.shape, mybir.dt.from_np(v.dtype), kind="ExternalInput").ap()
    out = nc.dram_tensor("out_0", (1, S, DM), F32, kind="ExternalOutput").ap()
    build(nc, args, out)
    r = _run(nc, [arrays], core_ids=[0])
    return r.results[0]["out_0"]
```
